# Optimizing a Trainium2 kernel written in Bass

```python
import numpy as np
import jax
import jax.numpy as jnp

def _softmax(x, axis=-1):
    return jax.nn.softmax(x, axis=axis)

def _gelu(x):
    return jax.nn.gelu(x, approximate=True)

def _silu(x):
    return jax.nn.silu(x)

def _sigmoid(x):
    return jax.nn.sigmoid(x)

def _layernorm(x, axis=-1, eps=1e-05):
    m = jnp.mean(x, axis=axis, keepdims=True)
    v = jnp.var(x, axis=axis, keepdims=True)
    return (x - m) / jnp.sqrt(v + eps)

def _scatter_add(tgt, idx, src, axis=0):
    return tgt.at[idx].add(src)

def _segment_sum(src, seg, n):
    return jax.ops.segment_sum(src, seg, n)
kernel_name = 'mk_gnn_preln_d1_gnn_r8_3d1fe4'

def setup_inputs(seed: int=0):
    np.random.seed(seed)
    _w = jnp.asarray

    def _rec_inputs():
        import jax
        import jax.numpy as jnp
        _gk = jax.random.key(seed)
        x = -0.0002117 + 1 * jax.random.normal(jax.random.fold_in(_gk, 1), (12500, 256), jnp.float32)
        src = jax.random.randint(jax.random.fold_in(_gk, 2), (200000,), 0, 12500, jnp.int32)
        dst = jax.random.randint(jax.random.fold_in(_gk, 3), (200000,), 0, 12500, jnp.int32)
        _o = jnp.argsort(dst, stable=True)
        src = src[_o]
        dst = dst[_o]
        return (x, src, dst)
    x, src, dst = _rec_inputs()

    def _L0_gnn_setup():
        import jax, jax.numpy as jnp
        import numpy as np
        N = 12500
        D = 256
        E = 37500
        BN_EPS = 1e-05

        def _batchnorm(x, gamma, beta):
            mean = jnp.mean(x, axis=0)
            var = jnp.var(x, axis=0)
            return (x - mean) * jax.lax.rsqrt(var + BN_EPS) * gamma + beta
        key = jax.random.key(seed)
        ks = jax.random.split(key, 8)
        h = jax.random.normal(ks[0], (N, D), dtype=jnp.float32)
        edge_index = jax.random.randint(ks[1], (2, E), 0, N, dtype=jnp.int64)
        W1 = jax.random.normal(ks[2], (D, 2 * D), dtype=jnp.float32) / np.sqrt(D)
        b1 = jnp.zeros((2 * D,), dtype=jnp.float32)
        g1 = jnp.ones((2 * D,), dtype=jnp.float32)
        bt1 = jnp.zeros((2 * D,), dtype=jnp.float32)
        W2 = jax.random.normal(ks[3], (2 * D, D), dtype=jnp.float32) / np.sqrt(2 * D)
        b2 = jnp.zeros((D,), dtype=jnp.float32)
        g2 = jnp.ones((D,), dtype=jnp.float32)
        bt2 = jnp.zeros((D,), dtype=jnp.float32)
        eps_gin = jnp.zeros((), dtype=jnp.float32)
        return {'h': h, 'edge_index': edge_index, 'W1': W1, 'b1': b1, 'g1': g1, 'bt1': bt1, 'W2': W2, 'b2': b2, 'g2': g2, 'bt2': bt2, 'eps_gin': eps_gin}
    _L0_gnn_all = _L0_gnn_setup()
    _L0_gnn_in = {k: v for k, v in _L0_gnn_all.items() if k in ('W1', 'b1', 'g1', 'bt1', 'W2', 'b2', 'g2', 'bt2', 'eps_gin')}
    del _L0_gnn_all
    return {'x': x, 'src': src, 'dst': dst, 'L0_gnn_W1': _L0_gnn_in['W1'], 'L0_gnn_b1': _L0_gnn_in['b1'], 'L0_gnn_g1': _L0_gnn_in['g1'], 'L0_gnn_bt1': _L0_gnn_in['bt1'], 'L0_gnn_W2': _L0_gnn_in['W2'], 'L0_gnn_b2': _L0_gnn_in['b2'], 'L0_gnn_g2': _L0_gnn_in['g2'], 'L0_gnn_bt2': _L0_gnn_in['bt2'], 'L0_gnn_eps_gin': _L0_gnn_in['eps_gin']}

def reference(x, src, dst, L0_gnn_W1, L0_gnn_b1, L0_gnn_g1, L0_gnn_bt1, L0_gnn_W2, L0_gnn_b2, L0_gnn_g2, L0_gnn_bt2, L0_gnn_eps_gin):
    import jax
    import jax.numpy as jnp

    def _L0_gnn_ref(h, edge_index, W1, b1, g1, bt1, W2, b2, g2, bt2, eps_gin):
        import jax, jax.numpy as jnp
        import numpy as np
        N = 12500
        D = 256
        E = 37500
        BN_EPS = 1e-05

        def _batchnorm(x, gamma, beta):
            mean = jnp.mean(x, axis=0)
            var = jnp.var(x, axis=0)
            return (x - mean) * jax.lax.rsqrt(var + BN_EPS) * gamma + beta
        src, dst = (edge_index[0], edge_index[1])
        agg = jax.ops.segment_sum(h[src], dst, num_segments=N)
        z = (1.0 + eps_gin) * h + agg
        t = jnp.dot(z, W1) + b1
        t = jax.nn.relu(_batchnorm(t, g1, bt1))
        conv_out = jnp.dot(t, W2) + b2
        out = jax.nn.relu(_batchnorm(conv_out + h, g2, bt2))
        return out
    edge_index = jnp.stack([src, dst])
    h = jnp.maximum(_layernorm(x, axis=-1), 0.0)
    x = x + _L0_gnn_ref(h, edge_index, L0_gnn_W1, L0_gnn_b1, L0_gnn_g1, L0_gnn_bt1, L0_gnn_W2, L0_gnn_b2, L0_gnn_g2, L0_gnn_bt2, L0_gnn_eps_gin)
    return x

_drawn_inputs = setup_inputs


def setup_inputs(seed=0):
    import zlib

    import numpy as np

    out = dict(_drawn_inputs(seed))
    spreads = {'L0_gnn_b1': (0.0, 0.8),
     'L0_gnn_g1': (1.0, 0.2),
     'L0_gnn_bt1': (0.0, 0.302),
     'L0_gnn_b2': (0.0, 0.8),
     'L0_gnn_g2': (1.0, 0.2),
     'L0_gnn_bt2': (0.0, 0.1)}
    factors = {}
    for name, (base, spread) in spreads.items():
        noise = np.random.default_rng([zlib.crc32(name.encode()), seed]).standard_normal(out[name].shape)
        drawn = base * np.exp(spread * noise) if base else spread * noise
        out[name] = jnp.asarray(drawn.astype(out[name].dtype))
    for name, factor in factors.items():
        out[name] = (out[name] * factor).astype(out[name].dtype)
    return out
```

```python
import concourse.bass as bass
from concourse import mybir
from contextlib import ExitStack

P = 128
D = 256
F = 512
DB, FB = D // P, F // P
GT = 4
GI = 4
SLOTS = GT * GI
W = 96
LN_EPS = BN_EPS = 1e-5
BANK = 512
Q = 4
QN = Q * P
XR = 4


def ceil(a, b):
    return -(-a // b)


def build(nc, x, src, dst, W1, b1, g1, bt1, W2, b2, g2, bt2, eps_gin, out):
    f32, i32 = mybir.dt.float32, mybir.dt.int32
    ALU = mybir.AluOpType
    ACT = mybir.ActivationFunctionType
    X = mybir.AxisListType.X
    N, E = x.shape[0], src.shape[0]

    NI = ceil(E, P * SLOTS)
    NT = ceil(N, P)
    assert NI == NT and NI >= 4 and N % 4 == 0 and NI * GI <= BANK
    LASTN = N - P * (NT - 1)
    NG, NE = NI * GI, NI * SLOTS
    EB = ceil(NE, P)
    FULLB = E // (P * P)
    RROWS = E // P - FULLB * P
    REDGE = E % P
    NZ = NT * P + W
    GW = max(w for w in range(1, BANK + 1) if N % w == 0)
    NW = N // GW
    LAG = 2
    NQF, NQ = N // QN, ceil(N, QN)
    TAILN = N - NQF * QN

    ctx = ExitStack()
    with ctx:
        def sb(name, shape, dt=f32):
            return ctx.enter_context(nc.sbuf_tensor(name, shape, dt))

        def sem(name):
            return ctx.enter_context(nc.semaphore(name))

        t_dram = nc.dram_tensor("t_and_h_T", (NT, P, (FB + DB) * P), f32, kind="Internal").ap()

        aggT = sb("aggT", [P, DB, NZ])
        ring = sb("ring", [P, (SLOTS + 2 * GT) * D])
        rows = ring[:, 0:SLOTS * D].rearrange("p (s d) -> p s d", d=D)
        hrow = ring[:, SLOTS * D:].rearrange("p (b s d) -> p b s d", b=2, d=D)
        tin = ring[:, 0:2 * Q * FB * P].rearrange("p (b c f n) -> p b c f n", b=2, c=Q, n=P)
        rl = ring[:, 0:2 * DB * QN].rearrange("p (b f n) -> p b f n", b=2, n=QN)
        work = sb("work", [P, 8192])
        tab_i = [work[:, n * EB * P:(n + 1) * EB * P].bitcast(i32).rearrange("p (b e) -> p b e", e=P) for n in (0, 1)]
        tab_f = [work[:, (2 + n) * EB * P:(3 + n) * EB * P].rearrange("p (b e) -> p b e", e=P) for n in (0, 1)]
        u = work[:, 0:4096].rearrange("p (b f n) -> p b f n", b=2, n=QN)
        xo = work[:, 4096:8192].rearrange("p (b k d) -> p b k d", b=XR, d=D)
        g_row, g_h = work[:, 0:D], work[:, D:2 * D]
        g_sel = work[:, 2 * D:2 * D + GW]
        g_iota = work[:, 1024:1024 + GW]
        g_dst = work[:, 1600:1601]
        g_stat, g_mv, g_nb = work[:, 1610:1616], work[:, 1620:1622], work[:, 1624:1625]
        g_idx = work[:, 1632:1633].bitcast(i32)
        HW = Q * DB * P
        tables = sb("tables", [P, max(2 * EB * P + NE, 2 * HW)])
        src_i = tables[:, 0:EB * P].bitcast(i32)
        dst_f = tables[:, EB * P:2 * EB * P]
        rel = tables[:, 2 * EB * P:2 * EB * P + NE]
        hin = [a.rearrange("p (c f n) -> p c f n", c=Q, n=P) for a in
               (ring[:, 4 * HW:5 * HW], ring[:, 5 * HW:6 * HW], tables[:, 0:HW], tables[:, HW:2 * HW])]
        rel_g = rel[:, :].rearrange("p (g k) -> p g k", k=GT)
        idx = sb("idx", [P, SLOTS], i32)
        base_f = sb("base_f", [P, NG])
        base_i = sb("base_i", [1, NG], i32)
        sched = sb("sched", [P, NG], i32)
        sel = sb("sel", [P, 2, GT, W])
        iota_w = sb("iota_w", [P, W])
        ident = sb("ident", [P, P])
        row0 = sb("row0", [P, P])
        prm = sb("prm", [18, P])
        prmT = sb("prmT", [P, 18])
        b1T, g1T, bt1T = prmT[:, 0:4], prmT[:, 4:8], prmT[:, 8:12]
        b2T, g2T, bt2T = prmT[:, 12:14], prmT[:, 14:16], prmT[:, 16:18]
        eps1 = sb("eps1", [P, 1])
        chk = sb("chk", [P, 4])
        flag_f = sb("flag_f", [1, 1])
        flag = sb("flag", [1, 1], i32)
        st = sb("st", [P, 2, GT, 6])
        mv = sb("mv", [P, 2, GT, 2])
        nb = sb("nb", [P, 2, GT])
        xt = sb("xt", [P, D])
        xst = sb("xst", [P, 6])
        xmv = sb("xmv", [P, 2])
        xnb = sb("xnb", [P, 1])
        hx = sb("hx", [P, D])
        zt = sb("zt", [P, DB, P])
        tb = sb("tb", [P, FB + DB, P])
        W1s = sb("W1s", [P, DB, F])
        W2s = sb("W2s", [P, FB, D])
        sts = sb("sts", [P, max(FB * NT, DB * NQ) * 6])
        st1 = sts[:, 0:FB * NT * 6].rearrange("p (f s) -> p f s", f=FB)
        st2 = sts[:, 0:DB * NQ * 6].rearrange("p (f s) -> p f s", f=DB)
        mv1 = sb("mv1", [P, FB, 2])
        sc1 = sb("sc1", [P, FB])
        sh1 = sb("sh1", [P, FB])
        tmp1 = sb("tmp1", [P, FB])
        mv2 = sb("mv2", [P, DB, 2])
        sc2 = sb("sc2", [P, DB])
        sh2 = sb("sh2", [P, DB])
        tmp2 = sb("tmp2", [P, DB])

        ps = ctx.enter_context(nc.psum_tensor("ps", [P, 8, BANK], f32))
        agg_ps = [ps[:, b, 0:DB * W].rearrange("p (f w) -> p f w", w=W) for b in (0, 1)]
        hT_ps = ps[:, 2, 0:D].rearrange("p (f n) -> p f n", n=P)
        t_ps = ps[:, 3, :].rearrange("p (f n) -> p f n", n=P)
        tr_ps = [ps[:, 4 + b, :] for b in (0, 1)]
        misc_ps = ps[:, 6, :]
        g_ps = ps[:, 6:8, :]
        c_ps = [[ps[:, 2 * b + f, :] for f in range(DB)] for b in (0, 1)]
        o_ps = [ps[:, 4 + 2 * b:6 + 2 * b, :] for b in (0, 1)]

        s_ident, s_iota, s_pad, s_zero, s_w = (sem(n) for n in ("s_ident", "s_iota", "s_pad", "s_zero", "s_w"))
        s_apart = sem("s_apart")
        s_tab = [sem("s_tab_src"), sem("s_tab_dst")]
        s_prm, s_par = sem("s_prm"), sem("s_par")
        s_tabf, s_tr, s_trc = sem("s_tabf"), sem("s_tr"), sem("s_trc")
        s_base, s_pre, s_flagT, s_flag = sem("s_base"), sem("s_pre"), sem("s_flagT"), sem("s_flag")
        s_gd, s_gi, s_gr, s_gs, s_gh, s_gm, s_gp, s_gv, s_gq, s_gend = (
            sem(n) for n in ("s_gd", "s_gi", "s_gr", "s_gs", "s_gh", "s_gm", "s_gp", "s_gv", "s_gq", "s_gend"))
        s_idx = sem("s_idx")
        s_rows = [sem(f"s_rows{j}") for j in range(GI)]
        s_bn, s_mv, s_sd, s_rstd, s_st, s_h, s_sel, s_agg, s_add = (
            sem(n) for n in ("s_bn", "s_mv", "s_sd", "s_rstd", "s_st", "s_h", "s_sel", "s_agg", "s_add"))
        s_xt, s_xbn, s_xmv, s_xsd, s_xrs, s_xst, s_hx, s_hT, s_hTc, s_zt, s_t, s_tb, s_tst, s_td = (
            sem(n) for n in ("s_xt", "s_xbn", "s_xmv", "s_xsd", "s_xrs", "s_xst", "s_hx", "s_hT", "s_hTc", "s_zt", "s_t",
                             "s_tb", "s_tst", "s_td"))
        s_bn1, s_bn2, s_root1, s_root2 = sem("s_bn1"), sem("s_bn2"), sem("s_root1"), sem("s_root2")
        s_tin = [sem(f"s_tin{b}") for b in range(2)]
        s_hin = [sem(f"s_hin{b}") for b in range(4)]
        s_u, s_c, s_y, s_yst = sem("s_u"), sem("s_c"), sem("s_y"), sem("s_yst")
        s_x = [sem(f"s_x{b}") for b in range(XR)]
        s_o = [sem(f"s_o{b}") for b in range(XR)]
        s_rl, s_oT, s_sum = sem("s_rl"), sem("s_oT"), sem("s_sum")

        NTR = 2 * ceil(EB, 4)
        ZP = NZ // 4

        def wait_apart(eng, s, value):
            eng.wait_ge(s, value)
            eng.sem_inc(s_apart, 1)

        def over(eng, first, n, body):
            for i in range(min(first, n)):
                body(i)
            if n > first:
                with eng.Fori(first, n) as i:
                    body(i)

        def chunks(eng, un, n_full, body, tail):
            rounds = n_full // un

            def round_(r):
                for k in range(un):
                    body(r * un + k, k, r)
            if rounds:
                over(eng, 1, rounds, round_)
            for q in range(rounds * un, n_full):
                body(q, q % un, q // un)
            if TAILN:
                tail(n_full, n_full % un, n_full // un)

        block = ctx.enter_context(nc.Block())

        @block.sync
        def _(sp):
            for n, a in enumerate((src, dst)):
                if FULLB:
                    sp.dma_start(tab_i[n][:, 0:FULLB, :], a[0:FULLB * P * P].rearrange("(b p e) -> p b e", p=P, e=P)
                                 ).then_inc(s_tab[n], 16)
            sp.wait_ge(s_pad, 2)
            for n, a in enumerate((src, dst)):
                at = FULLB * P * P
                if RROWS:
                    sp.dma_start(tab_i[n][0:RROWS, FULLB, :], a[at:at + RROWS * P].rearrange("(p e) -> p e", e=P)
                                 ).then_inc(s_tab[n], 16)
                if REDGE:
                    at += RROWS * P
                    sp.dma_start(tab_i[n][RROWS:RROWS + 1, FULLB, 0:REDGE], a[at:E].rearrange("(p e) -> p e", p=1)
                                 ).then_inc(s_tab[n], 16)
            r = 0
            for a in (b1, g1, bt1, b2, g2, bt2):
                k = a.shape[0] // P
                sp.dma_start(prm[r:r + k, :], a.rearrange("(r c) -> r c", c=P)).then_inc(s_prm, 16)
                r += k
            sp.dma_start(eps1[:, :], eps_gin.partition_broadcast(P)).then_inc(s_prm, 16)
            sp.dma_start(W1s[:, :, :], W1.rearrange("(k p) n -> p k n", p=P)).then_inc(s_w, 16)
            sp.dma_start(W2s[:, :, :], W2.rearrange("(k p) n -> p k n", p=P)).then_inc(s_w, 16)

            def load_node_tile(c, n=P):
                if not isinstance(c, int) or c > 0:
                    sp.wait_ge(s_hx, c)
                sp.dma_start(xt[0:n, :], x[bass.ds(c * P, n), :]).then_inc(s_xt, 16)

            def store_node_tile(c):
                sp.wait_ge(s_tb, c + 1)
                sp.dma_start(t_dram[bass.ds(c, 1), :, :].rearrange("c p f -> (c p) f"),
                             tb[:, :, :].rearrange("p f n -> p (f n)")).then_inc(s_td, 16)

            def node_tile(c):
                load_node_tile(c + 1)
                store_node_tile(c)
            load_node_tile(0)
            over(sp, 1, NT - 2, node_tile)
            load_node_tile(NT - 1, LASTN)
            store_node_tile(NT - 2)
            store_node_tile(NT - 1)
            sp.wait_ge(s_td, 16 * NT)
            sp.wait_ge(s_agg, NG)
            sp.wait_ge(s_sel, NG)

            def load_t(q, k, r, tiles=Q):
                if not isinstance(q, int) or q >= 2:
                    sp.wait_ge(s_u, q - 1)
                of = t_dram[bass.ds(q * Q, tiles), :, :].rearrange("c p f -> p c f")
                sp.dma_start(tin[:, k % 2, 0:tiles, :, :].rearrange("p c f n -> p c (f n)"),
                             of[:, :, 0:FB * P]).then_inc(s_tin[k % 2], 16)
                if not isinstance(q, int) or q >= 4:
                    sp.wait_ge(s_y, q - 3)
                sp.dma_start(hin[k][:, 0:tiles, :, :].rearrange("p c f n -> p c (f n)"),
                             of[:, :, FB * P:]).then_inc(s_hin[k], 16)

            def load_x(q, k, r, rows_=P):
                if not isinstance(q, int) or q >= XR:
                    sp.wait_ge(s_o[k], 16 * r)
                sp.dma_start(xo[0:rows_, k, :, :].rearrange("p k d -> p (k d)"),
                             x[bass.ds(q * QN, rows_ * 4), :].rearrange("(p k) d -> p (k d)", k=4)
                             ).then_inc(s_x[k], 16)
            early = min(XR, NQF)
            for q in range(early):
                load_x(q, q, 0)
            chunks(sp, 4, NQF, load_t, lambda q, k, r: load_t(q, k, r, ceil(TAILN, P)))

            def rest_x(r):
                for k in range(XR):
                    load_x(r * XR + k, k, r)
            full = NQF // XR
            if full > 1:
                with sp.Fori(1, full) as r:
                    rest_x(r)
            for q in range(max(full * XR, early), NQF):
                load_x(q, q % XR, q // XR)
            if TAILN:
                load_x(NQF, NQF % XR, NQF // XR, TAILN // 4)

        @block.gpsimd
        def _(pool):
            nc.gpsimd.memset(tab_i[0][:, EB - 1, :], 0).then_inc(s_pad, 1)
            nc.gpsimd.memset(tab_i[1][:, EB - 1, :], N).then_inc(s_pad, 1)
            nc.gpsimd.memset(ident[:, :], 0.0).then_inc(s_ident, 1)
            pool.wait_ge(s_ident, 1)
            nc.gpsimd.affine_select(out=ident[:, :], in_=ident[:, :], compare_op=ALU.not_equal, fill=1.0, base=0,
                                    pattern=[[-1, P]], channel_multiplier=1).then_inc(s_ident, 1)
            nc.gpsimd.iota(sched[:, :], pattern=[[P, NI], [0, GI]], base=P * (1 - LAG),
                           channel_multiplier=0).then_inc(s_iota, 1)
            nc.gpsimd.iota(iota_w[:, :], pattern=[[1, W]], base=0, channel_multiplier=0,
                           allow_small_or_imprecise_dtypes=True).then_inc(s_iota, 1)
            for f in range(DB):
                nc.gpsimd.memset(aggT[:, f, 0:ZP], 0.0).then_inc(s_zero, 1)

            def gather(i):
                for j in range(GI):
                    g = i * GI + j
                    if not isinstance(i, int) or i > 0:
                        pool.wait_ge(s_h, g - GI + 1)
                    wait_apart(pool, s_idx, g + 1)
                    for k in range(GT):
                        s = j * GT + k
                        nc.gpsimd.indirect_dma_start(
                            out=rows[:, s, :], out_offset=None, in_=x[:, :],
                            in_offset=bass.IndirectOffsetOnAxis(ap=idx[:, s:s + 1], axis=0)).then_inc(s_rows[j], 16)
            gather(0)
            pool.wait_ge(s_flag, 1)
            ok = pool.value_load(flag[0:1, 0:1], min_val=0, max_val=1)
            with pool.If(ok < 1):
                nc.gpsimd.iota(g_iota, pattern=[[1, GW]], base=0, channel_multiplier=0,
                               allow_small_or_imprecise_dtypes=True).then_inc(s_iota, 1)
                with pool.Fori(0, NE) as t:
                    wait_apart(pool, s_gi, t + 1)
                    nc.gpsimd.indirect_dma_start(
                        out=g_row, out_offset=None, in_=x[:, :],
                        in_offset=bass.IndirectOffsetOnAxis(ap=g_idx, axis=0)).then_inc(s_gr, 16)
            over(pool, 0, NI - 1, lambda i: gather(i + 1))

            def store_out(q, k, r, rows_=P):
                pool.wait_ge(s_sum, q + 1)
                nc.gpsimd.dma_start(out[bass.ds(q * QN, rows_ * 4), :].rearrange("(p k) d -> p (k d)", k=4),
                                    xo[0:rows_, k, :, :].rearrange("p k d -> p (k d)")).then_inc(s_o[k], 16)
            chunks(pool, XR, NQF, store_out, lambda q, k, r: store_out(q, k, r, TAILN // 4))
            for k in range(XR):
                pool.wait_ge(s_o[k], 16 * len(range(k, NQ, XR)))

        @block.vector
        def _(dve):
            V = nc.vector

            def partial_moments(rows_of, stats, s_stats):
                for r, o in zip(rows_of, stats):
                    last = V.bn_stats(o, r)
                last.then_inc(s_stats, 1)

            def moments(stats, mean_var, s_stats, s_mean, v):
                wait_apart(dve, s_stats, v)
                for o, m in zip(stats, mean_var):
                    last = V.bn_aggr(m, o)
                last.then_inc(s_mean, 1)

            def scale_and_shift(mean, std, shift, s_root, s_inv, s_done, v):
                dve.wait_ge(s_root, v)
                V.reciprocal(std, std).then_inc(s_inv, 1)
                dve.wait_ge(s_inv, v)
                V.scalar_tensor_tensor(shift, mean, -1.0, std, ALU.mult, ALU.mult).then_inc(s_done, 1)

            done = [0]

            def own(instruction):
                done[0] += 1
                instruction.then_inc(s_par, 1)
                dve.wait_ge(s_par, done[0])
            own(V.memset(row0[:, :], 0.0))
            own(V.memset(row0[0:1, :], 1.0))
            loads = 16 * (bool(FULLB) + bool(RROWS) + bool(REDGE))
            for n in (0, 1):
                dve.wait_ge(s_tab[n], loads)
                V.tensor_copy(tab_f[n], tab_i[n]).then_inc(s_tabf, 1)
                for b in range(NTR // 2):
                    w = min(4, EB - 4 * b) * P
                    k = n * (NTR // 2) + b
                    dve.wait_ge(s_tr, k + 1)
                    to = (src_i, dst_f)[n]
                    V.tensor_copy(to[:, 4 * b * P:4 * b * P + w], tr_ps[k % 2][:, 0:w]).then_inc(s_trc, 1)
                if n == 0:
                    dve.wait_ge(s_trc, NTR // 2)
                    V.tensor_copy(idx[:, :], src_i[:, 0:SLOTS]).then_inc(s_idx, GI)
            dve.wait_ge(s_base, 1)
            own(V.tensor_copy(base_f[:, :], misc_ps[:, 0:NG]))
            own(V.tensor_copy(base_i[:, :], misc_ps[0:1, 0:NG]))
            dve.wait_ge(s_iota, 2)
            own(V.tensor_tensor(rel_g, dst_f[:, 0:NE].rearrange("p (g k) -> p g k", k=GT),
                                base_f[:, :].unsqueeze(2).to_broadcast([P, NG, GT]), ALU.subtract))
            own(V.tensor_tensor(base_f[:, :], base_f[:, :], sched[:, :], ALU.subtract))
            own(V.tensor_reduce(chk[:, 3:4], rel[:, :], X, ALU.max))
            own(V.tensor_reduce(chk[:, 1:2], rel[:, :], X, ALU.min))
            own(V.tensor_reduce(chk[:, 2:3], base_f[:, :], X, ALU.min))
            own(V.tensor_scalar(chk[:, 0:1], chk[:, 3:4], -1.0, float(W - 1), ALU.mult, ALU.add))
            V.tensor_reduce(chk[:, 3:4], chk[:, 0:3], X, ALU.min).then_inc(s_pre, 1)
            dve.wait_ge(s_flagT, 1)
            own(V.tensor_copy(prmT[:, :], misc_ps[:, BANK - 18:BANK]))
            own(V.tensor_scalar(eps1[:, :], eps1[:, :], 1.0, None, ALU.add))
            dve.wait_ge(s_flagT, 2)
            own(V.tensor_reduce(flag_f[:, :], ps[0:1, 7, 0:P], X, ALU.min))
            V.tensor_scalar(flag[:, :], flag_f[:, :], 0.0, None, ALU.is_ge).then_inc(s_flag, 1)
            dve.wait_ge(s_flag, 1)
            ok = dve.value_load(flag[0:1, 0:1], min_val=0, max_val=1)
            dve.wait_ge(s_zero, 2 * DB)

            with dve.If(ok < 1):
                dve.wait_ge(s_iota, 3)
                V.memset(g_nb, 0.0).then_inc(s_gd, 1)
                with dve.Fori(0, NE) as t:
                    own = t * (4 + 2 * NW) + 1
                    dve.wait_ge(s_gd, own)
                    V.tensor_copy(g_idx, src_i[:, bass.ds(t, 1)]).then_inc(s_gi, 1)
                    V.tensor_copy(g_dst, dst_f[:, bass.ds(t, 1)]).then_inc(s_gd, 1)
                    dve.wait_ge(s_gr, 16 * t + 16)
                    V.bn_stats(g_stat, g_row).then_inc(s_gd, 1)
                    wait_apart(dve, s_gd, own + 2)
                    V.bn_aggr(g_mv, g_stat).then_inc(s_gv, 1)
                    dve.wait_ge(s_gq, t + 1)
                    V.reciprocal(g_mv[:, 1:2], g_mv[:, 1:2]).then_inc(s_gd, 1)
                    dve.wait_ge(s_gd, own + 3)
                    V.scalar_tensor_tensor(g_nb, g_mv[:, 0:1], -1.0, g_mv[:, 1:2], ALU.mult, ALU.mult).then_inc(s_gs, 1)
                    dve.wait_ge(s_gh, t + 1)
                    V.memset(g_nb, 0.0).then_inc(s_gd, 1)
                    with dve.Fori(0, NW) as w:
                        n = t * NW + w
                        dve.wait_ge(s_gd, own + 4 + 2 * w)
                        V.tensor_tensor(g_sel, g_iota, g_dst.to_broadcast([P, GW]), ALU.is_equal).then_inc(s_gm, 1)
                        dve.wait_ge(s_gm, n + 1)
                        V.tensor_scalar(g_dst, g_dst, float(-GW), None, ALU.add).then_inc(s_gd, 1)
                        dve.wait_ge(s_gp, n + 1)
                        z = aggT[:, :, bass.ds(w * GW, GW)]
                        V.tensor_tensor(z, z, g_ps[:, :, 0:GW], ALU.add).then_inc(s_gd, 1)
                V.memset(rel[:, :], -1.0).then_inc(s_gend, 1)
                V.memset(base_i[:, :], 0).then_inc(s_gend, 1)
                dve.wait_ge(s_gend, 2)
                dve.wait_ge(s_gd, NE * (4 + 2 * NW) + 1)

            def statistics(i, j):
                dve.wait_ge(s_rows[j], 64 * i + 64)
                partial_moments([rows[:, j * GT + k, :] for k in range(GT)], [st[:, j % 2, k, :] for k in range(GT)],
                                s_bn)

            def mean_and_var(i, j):
                g, r = i * GI + j, j % 2
                if not isinstance(g, int) or g >= 2:
                    dve.wait_ge(s_h, g - 1)
                moments([st[:, r, k, :] for k in range(GT)], [mv[:, r, k, :] for k in range(GT)], s_bn, s_mv, g + 1)

            def scale(i, j):
                r = j % 2
                scale_and_shift(mv[:, r, :, 0], mv[:, r, :, 1], nb[:, r, :], s_sd, s_rstd, s_st, i * GI + j + 1)

            def selection(i, j):
                g = i * GI + j
                V.tensor_tensor(sel[:, j % 2, :, :],
                                rel[:, bass.ds(g * GT, GT)].unsqueeze(2).to_broadcast([P, GT, W]),
                                iota_w[:, :].unsqueeze(1).to_broadcast([P, GT, W]), ALU.is_equal).then_inc(s_sel, 1)

            def next_rows(i, j):
                V.tensor_copy(idx[:, j * GT:(j + 1) * GT],
                              src_i[:, bass.ds((i + 1) * SLOTS + j * GT, GT)]).then_inc(s_idx, 1)

            def add_window(g, r):
                at = dve.value_load(base_i[0:1, bass.ds(g, 1)], min_val=0, max_val=N)
                dve.wait_ge(s_agg, g + 1)
                if not isinstance(g, int) or g > 0:
                    dve.wait_ge(s_add, g)
                z = aggT[:, :, bass.ds(at, W)]
                V.tensor_tensor(z, z, agg_ps[r], ALU.add).then_inc(s_add, 1)

            def statistics_node_tile(c, n=P):
                dve.wait_ge(s_xt, 16 * c + 16)
                partial_moments([xt[0:n, :]], [xst[0:n, :]], s_xbn)

            def mean_and_var_node_tile(c, n=P):
                moments([xst[0:n, :]], [xmv[0:n, :]], s_xbn, s_xmv, c + 1)

            def scale_node_tile(c, n=P):
                scale_and_shift(xmv[0:n, 0:1], xmv[0:n, 1:2], xnb[0:n, :], s_xsd, s_xrs, s_xst, c + 1)

            def z_tile(c, added, n=P):
                dve.wait_ge(s_hTc, c + 1)
                dve.wait_ge(s_add, added)
                if not isinstance(c, int) or c > 0:
                    dve.wait_ge(s_t, c)
                V.scalar_tensor_tensor(zt[:, :, 0:n], tb[:, FB:FB + DB, 0:n], eps1[:, 0:1], aggT[:, :, bass.ds(c * P, n)],
                                       ALU.mult, ALU.add).then_inc(s_zt, 1)

            def t_stats(c, n=P):
                dve.wait_ge(s_tb, c + 1)
                for f in range(FB):
                    last = V.bn_stats(st1[:, f, bass.ds(c * 6, 6)], tb[:, f, 0:n])
                last.then_inc(s_tst, 1)

            def iteration(i):
                c = i - LAG
                tiles, tiles_before = not isinstance(i, int) or i >= LAG, not isinstance(i, int) or i > LAG
                for j in range(GI):
                    statistics(i, j)
                    if tiles and j == 0:
                        statistics_node_tile(c)
                    if not isinstance(i, int) or i * GI + j >= 2:
                        add_window(i * GI + j - 2, j % 2)
                    mean_and_var(i, j)
                    if tiles and j == 0:
                        mean_and_var_node_tile(c)
                    selection(i, j)
                    if not (isinstance(i, int) and i == NI - 1):
                        next_rows(i, j)
                    if tiles_before and j == 1:
                        t_stats(c - 1)
                    scale(i, j)
                    if tiles and j == 0:
                        scale_node_tile(c)
                    if tiles and j == 2:
                        z_tile(c, i * GI)
            over(dve, LAG + 1, NI - 1, iteration)
            iteration(NI - 1)
            add_window(NG - 2, 0)
            add_window(NG - 1, 1)
            t_stats(NT - 3)
            for c, n in ((NT - 2, P), (NT - 1, LASTN)):
                statistics_node_tile(c, n)
                mean_and_var_node_tile(c, n)
                scale_node_tile(c, n)
                z_tile(c, NG, n)
                t_stats(c, n)

            def batch_norm(stats_, mean_var, gT, btT, scale, shift, tmp, blocks, s_own, s_root, s_stats, v):
                dve.wait_ge(s_stats, v)
                for f in range(blocks):
                    last = V.bn_aggr(mean_var[:, f, :], stats_[:, f, :])
                last.then_inc(s_own, 1)
                dve.wait_ge(s_root, 1)
                V.reciprocal(tmp[:, :], tmp[:, :]).then_inc(s_own, 1)
                dve.wait_ge(s_own, 2)
                V.tensor_tensor(scale[:, :], tmp[:, :], gT, ALU.mult).then_inc(s_own, 1)
                dve.wait_ge(s_own, 3)
                V.tensor_tensor(tmp[:, :], mean_var[:, :, 0], scale[:, :], ALU.mult).then_inc(s_own, 1)
                dve.wait_ge(s_own, 4)
                V.tensor_tensor(shift[:, :], btT, tmp[:, :], ALU.subtract).then_inc(s_own, 1)
            batch_norm(st1, mv1, g1T, bt1T, sc1, sh1, tmp1, FB, s_bn1, s_root1, s_tst, NT)

            def y_chunk(q, k, r, n=QN):
                dve.wait_ge(s_hin[k], 16 * r + 16)
                dve.wait_ge(s_c, q + 1)
                tiles = ceil(n, P)
                for f in range(DB):
                    for a, b, t0, t1 in (((0, n, 0, tiles),) if n % P == 0 else
                                         ((0, n - n % P, 0, tiles - 1), (n - n % P, n, tiles - 1, tiles))):
                        if a == b:
                            continue
                        w = min(P, b - a)
                        last = V.scalar_tensor_tensor(
                            aggT[:, f, bass.ds(q * QN + a, b - a)].rearrange("p (c n) -> p c n", n=w),
                            c_ps[k % 2][f][:, a:b].rearrange("p (c n) -> p c n", n=w), b2T[:, f:f + 1],
                            hin[k][:, t0:t1, f, 0:w], ALU.add, ALU.add)
                last.then_inc(s_y, 1)
                dve.wait_ge(s_y, q + 1)
                for f in range(DB):
                    last = V.bn_stats(st2[:, f, bass.ds(q * 6, 6)], aggT[:, f, bass.ds(q * QN, n)])
                last.then_inc(s_yst, 1)
            chunks(dve, 4, NQF, y_chunk, lambda q, k, r: y_chunk(q, k, r, TAILN))
            batch_norm(st2, mv2, g2T, bt2T, sc2, sh2, tmp2, DB, s_bn2, s_root2, s_yst, NQ)

            def residual(q, k, r, rows_=P):
                dve.wait_ge(s_x[k], 16 * r + 16)
                dve.wait_ge(s_oT, q + 1)
                V.tensor_tensor(xo[0:rows_, k, :, :].rearrange("p k d -> p (k d)"),
                                o_ps[k % 2][0:rows_, :, :].rearrange("p b n -> p (b n)"),
                                xo[0:rows_, k, :, :].rearrange("p k d -> p (k d)"), ALU.add).then_inc(s_sum, 1)
            chunks(dve, XR, NQF, residual, lambda q, k, r: residual(q, k, r, TAILN // 4))

        @block.scalar
        def _(act):
            S = nc.scalar
            for f in range(DB):
                S.memzero(aggT[:, f, ZP:NZ]).then_inc(s_zero, 1)
            act.wait_ge(s_flag, 1)
            ok = act.value_load(flag[0:1, 0:1], min_val=0, max_val=1)
            with act.If(ok < 1):
                with act.Fori(0, NE) as t:
                    act.wait_ge(s_gv, t + 1)
                    S.activation(g_mv[:, 1:2], g_mv[:, 1:2], ACT.Sqrt, bias=LN_EPS).then_inc(s_gq, 1)
                    act.wait_ge(s_gs, t + 1)
                    S.activation(g_h, g_row, ACT.Relu, bias=g_nb, scale=g_mv[:, 1:2]).then_inc(s_gh, 1)
                act.wait_ge(s_gend, 2)

            def root(i, j):
                act.wait_ge(s_mv, i * GI + j + 1)
                var = mv[:, j % 2, :, 1]
                S.activation(var, var, ACT.Sqrt, bias=LN_EPS).then_inc(s_sd, 1)

            def root_node_tile(c, n=P):
                act.wait_ge(s_xmv, c + 1)
                S.activation(xmv[0:n, 1:2], xmv[0:n, 1:2], ACT.Sqrt, bias=LN_EPS).then_inc(s_xsd, 1)

            def normalise(i, j):
                g, r = i * GI + j, j % 2
                act.wait_ge(s_st, g + 1)
                if not isinstance(g, int) or g >= 2:
                    act.wait_ge(s_agg, g - 1)
                for k in range(GT):
                    last = S.activation(hrow[:, r, k, :], rows[:, j * GT + k, :], ACT.Relu,
                                        bias=nb[:, r, k:k + 1], scale=mv[:, r, k, 1:2])
                last.then_inc(s_h, 1)

            def norm_node_tile(c, n=P):
                act.wait_ge(s_xst, c + 1)
                if not isinstance(c, int) or c > 0:
                    act.wait_ge(s_hT, c)
                S.activation(hx[0:n, :], xt[0:n, :], ACT.Relu, bias=xnb[0:n, :], scale=xmv[0:n, 1:2]).then_inc(s_hx, 1)

            def copy_hT(c, n=P):
                act.wait_ge(s_hT, c + 1)
                if not isinstance(c, int) or c > 0:
                    act.wait_ge(s_td, 16 * c)
                S.copy(tb[:, FB:FB + DB, 0:n], hT_ps[:, :, 0:n]).then_inc(s_hTc, 1)

            def t_and_b1(c, n=P):
                act.wait_ge(s_t, c + 1)
                if not isinstance(c, int) or c > 0:
                    act.wait_ge(s_tst, c)
                for f in range(FB):
                    last = S.activation(tb[:, f, 0:n], t_ps[:, f, 0:n], ACT.Identity, bias=b1T[:, f:f + 1], scale=1.0)
                last.then_inc(s_tb, 1)

            def iteration(i):
                c = i - LAG
                tiles = not isinstance(i, int) or i >= LAG
                for j in range(GI):
                    root(i, j)
                    if tiles and j == 0:
                        root_node_tile(c)
                    normalise(i, j)
                    if tiles and j == 0:
                        norm_node_tile(c)
                    if tiles and j == 1:
                        copy_hT(c)
                    if tiles and j == 3:
                        t_and_b1(c)
            over(act, LAG, NI, iteration)
            for c, n in ((NT - 2, P), (NT - 1, LASTN)):
                root_node_tile(c, n)
                norm_node_tile(c, n)
                copy_hT(c, n)
                t_and_b1(c, n)

            def batch_root(mean_var, tmp, s_own, s_root):
                act.wait_ge(s_own, 1)
                S.activation(tmp[:, :], mean_var[:, :, 1], ACT.Sqrt, bias=BN_EPS).then_inc(s_root, 1)
            batch_root(mv1, tmp1, s_bn1, s_root1)
            act.wait_ge(s_bn1, 5)

            def relu1(q, k, r, tiles=Q):
                act.wait_ge(s_tin[k % 2], 32 * r + 16 * (k // 2) + 16)
                if not isinstance(q, int) or q >= 2:
                    act.wait_ge(s_c, q - 1)
                for f in range(FB):
                    last = S.activation(u[:, k % 2, f, 0:tiles * P].rearrange("p (c n) -> p c n", n=P),
                                        tin[:, k % 2, 0:tiles, f, :], ACT.Relu, bias=sh1[:, f:f + 1],
                                        scale=sc1[:, f:f + 1])
                last.then_inc(s_u, 1)
            chunks(act, 4, NQF, relu1, lambda q, k, r: relu1(q, k, r, ceil(TAILN, P)))
            batch_root(mv2, tmp2, s_bn2, s_root2)
            act.wait_ge(s_bn2, 5)

            def relu2(q, k, r, n=QN):
                if not isinstance(q, int) or q >= 2:
                    act.wait_ge(s_oT, q - 1)
                for f in range(DB):
                    last = S.activation(rl[:, k % 2, f, 0:n], aggT[:, f, bass.ds(q * QN, n)], ACT.Relu,
                                        bias=sh2[:, f:f + 1], scale=sc2[:, f:f + 1])
                last.then_inc(s_rl, 1)
            chunks(act, XR, NQF, relu2, lambda q, k, r: relu2(q, k, r, TAILN))

        @block.tensor
        def _(pe):
            T = nc.tensor
            pe.wait_ge(s_ident, 2)
            for n in (0, 1):
                pe.wait_ge(s_tabf, n + 1)
                for b in range(NTR // 2):
                    k = n * (NTR // 2) + b
                    if k >= 2:
                        pe.wait_ge(s_trc, k - 1)
                    for m in range(min(4, EB - 4 * b)):
                        last = T.transpose(tr_ps[k % 2][:, m * P:(m + 1) * P], tab_f[n][:, 4 * b + m, :], ident[:, :])
                    last.then_inc(s_tr, 1)
            pe.wait_ge(s_trc, NTR)
            pe.wait_ge(s_par, 2)
            T.matmul(misc_ps[:, 0:NG], row0[:, :], dst_f[:, 0:NE:GT], start=True, stop=True).then_inc(s_base, 1)
            pe.wait_ge(s_prm, 16 * 7)
            pe.wait_ge(s_pre, 1)
            T.transpose(misc_ps[:, BANK - 18:BANK], prm[:, :], ident[0:18, 0:18]).then_inc(s_flagT, 1)
            T.transpose(ps[0:1, 7, 0:P], chk[:, 3:4], ident[:, :]).then_inc(s_flagT, 1)
            pe.wait_ge(s_flag, 1)
            ok = pe.value_load(flag[0:1, 0:1], min_val=0, max_val=1)
            with pe.If(ok < 1):
                with pe.Fori(0, NE) as t:
                    wait_apart(pe, s_gh, t + 1)
                    with pe.Fori(0, NW) as w:
                        pe.wait_ge(s_gm, t * NW + w + 1)
                        for f in range(DB):
                            last = T.matmul(g_ps[:, f, 0:GW], g_h[:, f * P:(f + 1) * P], g_sel, start=True, stop=True)
                        last.then_inc(s_gp, 1)
                pe.wait_ge(s_gend, 2)

            def aggregate(i, j):
                g, r = i * GI + j, j % 2
                pe.wait_ge(s_h, g + 1)
                pe.wait_ge(s_sel, g + 1)
                if not isinstance(g, int) or g >= 2:
                    pe.wait_ge(s_add, g - 1)
                for f in range(DB):
                    for k in range(GT):
                        last = T.matmul(agg_ps[r][:, f, :], hrow[:, r, k, f * P:(f + 1) * P], sel[:, r, k, :],
                                        start=k == 0, stop=k == GT - 1)
                last.then_inc(s_agg, 1)

            def transpose_h(c, n=P):
                pe.wait_ge(s_hx, c + 1)
                if not isinstance(c, int) or c > 0:
                    pe.wait_ge(s_hTc, c)
                for f in range(DB):
                    last = T.transpose(hT_ps[:, f, 0:n], hx[0:n, f * P:(f + 1) * P], ident[0:n, 0:n])
                last.then_inc(s_hT, 1)

            def times_W1(c, n=P):
                pe.wait_ge(s_zt, c + 1)
                if not isinstance(c, int) or c > 0:
                    pe.wait_ge(s_tb, c)
                for m in range(FB):
                    for k in range(DB):
                        last = T.matmul(t_ps[:, m, 0:n], W1s[:, k, m * P:(m + 1) * P], zt[:, k, 0:n],
                                        start=k == 0, stop=k == DB - 1)
                last.then_inc(s_t, 1)

            def iteration(i):
                c = i - LAG
                tiles = not isinstance(i, int) or i >= LAG
                for j in range(GI):
                    aggregate(i, j)
                    if tiles and j == 0:
                        transpose_h(c)
                    if tiles and j == 2:
                        times_W1(c)
            pe.wait_ge(s_w, 32)
            over(pe, LAG, NI, iteration)
            for c, n in ((NT - 2, P), (NT - 1, LASTN)):
                transpose_h(c, n)
                times_W1(c, n)

            def times_W2(q, k, r, n=QN):
                pe.wait_ge(s_u, q + 1)
                if not isinstance(q, int) or q >= 2:
                    pe.wait_ge(s_y, q - 1)
                for m in range(DB):
                    for f in range(FB):
                        last = T.matmul(c_ps[k % 2][m][:, 0:n], W2s[:, f, m * P:(m + 1) * P], u[:, k % 2, f, 0:n],
                                        start=f == 0, stop=f == FB - 1)
                last.then_inc(s_c, 1)
            chunks(pe, 4, NQF, times_W2, lambda q, k, r: times_W2(q, k, r, TAILN))

            def transpose_out(q, k, r, n=QN):
                pe.wait_ge(s_rl, q + 1)
                if not isinstance(q, int) or q >= 2:
                    pe.wait_ge(s_sum, q - 1)
                for m in range(4):
                    for f in range(DB):
                        at = (m % 2) * D + f * P
                        last = T.transpose(o_ps[k % 2][0:n // 4, m // 2, at:at + P], rl[:, k % 2, f, m:n:4],
                                           ident[:, :])
                last.then_inc(s_oT, 1)
            chunks(pe, XR, NQF, transpose_out, lambda q, k, r: transpose_out(q, k, r, TAILN))


_INS = ["x", "src", "dst", "L0_gnn_W1", "L0_gnn_b1", "L0_gnn_g1", "L0_gnn_bt1", "L0_gnn_W2", "L0_gnn_b2",
        "L0_gnn_g2", "L0_gnn_bt2", "L0_gnn_eps_gin"]


def kernel(**inputs):
    import numpy as np
    import concourse.bacc as bacc
    from concourse.bass_utils import run_bass_kernel_spmd

    nc = bacc.Bacc("TRN2", target_bir_lowering=False, num_devices=1)
    arrays, args = {}, []
    for name in _INS:
        a = np.ascontiguousarray(inputs[name])
        if name.endswith("eps_gin"):
            a = a.reshape(1, 1)
        arrays[f"in_{name}"] = a
        args.append(nc.dram_tensor(f"in_{name}", a.shape, mybir.dt.from_np(a.dtype), kind="ExternalInput").ap())
    out = nc.dram_tensor("out", inputs["x"].shape, mybir.dt.float32, kind="ExternalOutput").ap()
    build(nc, *args, out)
    r = run_bass_kernel_spmd(nc, [arrays], core_ids=[0])
    return r.results[0]["out"]
```

```python
import concourse.bass as bass
from concourse import mybir
from contextlib import ExitStack

P = 128
D = 256
F = 512
DB, FB = D // P, F // P
GT = 4
GI = 4
SLOTS = GT * GI
W = 96
HALF = (W - 1) / 2
LN_EPS = BN_EPS = 1e-5
BANK = 512
Q = 4
QN = Q * P
XU = 8
XW = Q * D
X_EARLY = 14


def ceil(a, b):
    return -(-a // b)


def build(nc, x, src, dst, W1, b1, g1, bt1, W2, b2, g2, bt2, eps_gin, out):
    f32, i32 = mybir.dt.float32, mybir.dt.int32
    ALU = mybir.AluOpType
    ACT = mybir.ActivationFunctionType
    X = mybir.AxisListType.X
    N, E = x.shape[0], src.shape[0]

    NI = ceil(E, P * SLOTS)
    NT = ceil(N, P)
    assert NI == NT and NI >= 4 and N % 4 == 0 and NI * GI <= BANK
    LASTN = N - P * (NT - 1)
    NG, NE = NI * GI, NI * SLOTS
    TILES = ceil(E, P)
    GROUPS = ceil(TILES, GT)
    EB = ceil(NE, P)
    FULLB = E // (P * P)
    RROWS = E // P - FULLB * P
    REDGE = E % P
    NZ = NT * P + W
    GW = max(w for w in range(1, BANK + 1) if N % w == 0)
    NW = N // GW
    LAG = 2
    NQF, NQ = N // QN, ceil(N, QN)
    TAILN = N - NQF * QN

    ctx = ExitStack()
    with ctx:
        def sb(name, shape, dt=f32):
            return ctx.enter_context(nc.sbuf_tensor(name, shape, dt))

        def sem(name):
            return ctx.enter_context(nc.semaphore(name))

        t_dram = nc.dram_tensor("t_and_h_T", (NT, P, (FB + DB) * P), f32, kind="Internal").ap()

        aggT = sb("aggT", [P, DB, NZ])
        n_st1, n_w1, n_sel, n_tb, n_zt = max(FB * NT * 6, 512 + 2 * NG), DB * F, 2 * GT * W, FB * P, DB * P
        ONCE = [n_st1, n_w1, n_sel, n_tb, n_zt, D, D, DB * P]
        MAIN = [sum(ONCE), 8192, 2 * EB * P + NE, (SLOTS + 2 * GT) * D]
        U_AT = X_EARLY * XW
        TIN_AT = U_AT + 2 * FB * QN
        HIN_AT = TIN_AT + 2 * Q * FB * P
        ST2_AT = HIN_AT + 2 * Q * DB * P
        assert TIN_AT >= sum(MAIN[:2])
        assert NQF * XW <= ST2_AT
        arena = sb("arena", [P, max(sum(MAIN), ST2_AT + DB * NQ * 6)])
        once, work, tables, ring = (arena[:, sum(MAIN[:n]):sum(MAIN[:n + 1])] for n in range(4))
        u = arena[:, U_AT:TIN_AT].rearrange("p (b f n) -> p b f n", b=2, n=QN)
        tin = arena[:, TIN_AT:HIN_AT].rearrange("p (b c f n) -> p b c f n", b=2, c=Q, n=P)
        hin = arena[:, HIN_AT:ST2_AT].rearrange("p (b c f n) -> p b c f n", b=2, c=Q, n=P)
        st2 = arena[:, ST2_AT:ST2_AT + DB * NQ * 6].rearrange("p (f s) -> p f s", f=DB)
        rows = ring[:, 0:SLOTS * D].rearrange("p (s d) -> p s d", d=D)
        hrow = ring[:, SLOTS * D:].rearrange("p (b s d) -> p b s d", b=2, d=D)
        tab_i = [work[:, n * EB * P:(n + 1) * EB * P].bitcast(i32).rearrange("p (b e) -> p b e", e=P) for n in (0, 1)]
        tab_f = [work[:, (2 + n) * EB * P:(3 + n) * EB * P].rearrange("p (b e) -> p b e", e=P) for n in (0, 1)]
        piece = [once[:, sum(ONCE[:n]):sum(ONCE[:n + 1])] for n in range(len(ONCE))]
        g_row, g_h = work[:, 0:D], work[:, D:2 * D]
        g_sel = work[:, 2 * D:2 * D + GW]
        g_iota = work[:, 1024:1024 + GW]
        g_dst = work[:, 1600:1601]
        g_stat, g_mv, g_nb = work[:, 1610:1616], work[:, 1620:1622], work[:, 1624:1625]
        g_idx = work[:, 1632:1633].bitcast(i32)
        src_i = tables[:, 0:EB * P].bitcast(i32)
        dst_f = tables[:, EB * P:2 * EB * P]
        rel = tables[:, 2 * EB * P:2 * EB * P + NE]
        rel_g = rel.rearrange("p (g k) -> p g k", k=GT)
        idx = sb("idx", [P, SLOTS], i32)
        base_i = sb("base_i", [1, NG], i32)
        sel = piece[2].rearrange("p (b k w) -> p b k w", b=2, w=W)
        early_ = piece[0]
        first_i = early_[0:SLOTS, 0:P].bitcast(i32)
        first_f = early_[0:SLOTS, P:2 * P]
        row0 = early_[:, 2 * P:3 * P]
        base_f = early_[:, 384:384 + NG]
        sched = early_[:, 384 + NG:384 + 2 * NG].bitcast(i32)
        iota_w = sb("iota_w", [P, W])
        ident = sb("ident", [P, P])
        prm = early_[0:18, 384 + 2 * NG:384 + 2 * NG + P]
        prmT = sb("prmT", [P, 18])
        b1T, g1T, bt1T = prmT[:, 0:4], prmT[:, 4:8], prmT[:, 8:12]
        b2T, g2T, bt2T = prmT[:, 12:14], prmT[:, 14:16], prmT[:, 16:18]
        eps1 = sb("eps1", [P, 1])
        chk = sb("chk", [P, 4])
        flag_f = sb("flag_f", [1, 1])
        flag = sb("flag", [1, 1], i32)
        st = sb("st", [P, 2, GT, 6])
        mv = sb("mv", [P, 2, GT, 2])
        nb = sb("nb", [P, 2, GT])
        xt = piece[5]
        xst = sb("xst", [P, 6])
        xmv = sb("xmv", [P, 2])
        xnb = sb("xnb", [P, 1])
        hx = piece[6]
        hTs = [a.rearrange("p (f n) -> p f n", n=P) for a in (piece[7], work[:, n_zt + n_tb:2 * n_zt + n_tb])]
        zt = [a.rearrange("p (f n) -> p f n", n=P) for a in (piece[4], work[:, 0:n_zt])]
        tb = [a.rearrange("p (f n) -> p f n", n=P) for a in (piece[3], work[:, n_zt:n_zt + n_tb])]
        W1s = piece[1].rearrange("p (k n) -> p k n", n=F)
        W2s = sb("W2s", [P, FB, D])
        st1 = piece[0][:, 0:FB * NT * 6].rearrange("p (f s) -> p f s", f=FB)
        x_tail = aggT[:, :, 0:QN]
        rl = [W2s.rearrange("p f d -> p (f d)").rearrange("p (f n) -> p f n", n=QN),
              sb("rl_odd", [P, DB, QN])]
        mv1 = sb("mv1", [P, FB, 2])
        sc1 = sb("sc1", [P, FB])
        sh1 = sb("sh1", [P, FB])
        tmp1 = sb("tmp1", [P, FB])
        mv2 = sb("mv2", [P, DB, 2])
        sc2 = sb("sc2", [P, DB])
        sh2 = sb("sh2", [P, DB])
        tmp2 = sb("tmp2", [P, DB])

        ps = ctx.enter_context(nc.psum_tensor("ps", [P, 8, BANK], f32))
        agg_ps = [ps[:, b, 0:DB * W].rearrange("p (f w) -> p f w", w=W) for b in (0, 1)]
        hT_ps = ps[:, 2, 0:D].rearrange("p (f n) -> p f n", n=P)
        t_ps = [ps[:, b, :].rearrange("p (f n) -> p f n", n=P) for b in (3, 4)]
        tr_ps = [[ps[:, 2 + b, :] for b in (0, 1)], [ps[:, 4 + b, :] for b in (0, 1)]]
        misc_ps = ps[:, 6, :]
        prm_ps = ps[:, 7, 0:18]
        flag_ps = ps[0:1, 5, 0:P]
        g_ps = ps[:, 6:8, :]
        c_ps = [[ps[:, 2 * b + f, :] for f in range(DB)] for b in (0, 1)]
        o_ps = [ps[:, 4 + 2 * b:6 + 2 * b, :] for b in (0, 1)]

        s_ident, s_iota, s_pad, s_zero, s_w = (sem(n) for n in ("s_ident", "s_iota", "s_pad", "s_zero", "s_w"))
        s_apart = sem("s_apart")
        s_first, s_firstf, s_firstT = sem("s_first"), sem("s_firstf"), sem("s_firstT")
        s_tab = [sem("s_tab_src"), sem("s_tab_dst")]
        s_prm, s_par = sem("s_prm"), sem("s_par")
        s_tabf, s_tr, s_trc = ([sem(f"{a}_{b}") for b in ("src", "dst")] for a in ("s_tabf", "s_tr", "s_trc"))
        s_base, s_pre, s_flagT, s_flag = sem("s_base"), sem("s_pre"), sem("s_flagT"), sem("s_flag")
        s_gd, s_gi, s_gr, s_gs, s_gh, s_gm, s_gp, s_gv, s_gq, s_gend = (
            sem(n) for n in ("s_gd", "s_gi", "s_gr", "s_gs", "s_gh", "s_gm", "s_gp", "s_gv", "s_gq", "s_gend"))
        s_idx = sem("s_idx")
        s_rows = [sem(f"s_rows{j}") for j in range(GI)]
        s_bn, s_mv, s_sd, s_rstd, s_st, s_h, s_sel, s_agg, s_add = (
            sem(n) for n in ("s_bn", "s_mv", "s_sd", "s_rstd", "s_st", "s_h", "s_sel", "s_agg", "s_add"))
        s_xt, s_xbn, s_xmv, s_xsd, s_xrs, s_xst, s_hx, s_hT, s_hTc, s_zt, s_t, s_tb, s_tst, s_td, s_hs = (
            sem(n) for n in ("s_xt", "s_xbn", "s_xmv", "s_xsd", "s_xrs", "s_xst", "s_hx", "s_hT", "s_hTc", "s_zt", "s_t",
                             "s_tb", "s_tst", "s_td", "s_hs"))
        s_bn1, s_bn2, s_root1, s_root2 = sem("s_bn1"), sem("s_bn2"), sem("s_root1"), sem("s_root2")
        s_tin = [sem(f"s_tin{b}") for b in range(2)]
        s_hin = [sem(f"s_hin{b}") for b in range(2)]
        s_u, s_c, s_y, s_yst = sem("s_u"), sem("s_c"), sem("s_y"), sem("s_yst")
        s_x = [sem(f"s_x{b}") for b in range(XU)]
        s_o = sem("s_o")
        s_rl, s_oT, s_sum = sem("s_rl"), sem("s_oT"), sem("s_sum")

        NTR = ceil(EB, 4)
        ZP, ZW = NZ // 24, NZ // 32
        ZV = ZP + 16 * ZW
        ZA = [ZV, ZV + NZ // 4, NZ]

        def wait_apart(eng, s, value):
            eng.wait_ge(s, value)
            eng.sem_inc(s_apart, 1)

        def tiles_of(i, j):
            return GT if not isinstance(i, int) or i < NI - 1 else max(0, min(GT, TILES - (i * GI + j) * GT))

        TAB_LOADS = 16 * (bool(FULLB) + bool(RROWS) + bool(REDGE))

        def at_least(i, least):
            return not isinstance(i, int) or i >= least

        def over(eng, first, n, body):
            for i in range(min(first, n)):
                body(i)
            if n > first:
                with eng.Fori(first, n) as i:
                    body(i)

        def chunks(eng, un, n_full, body, tail):
            rounds = n_full // un

            def round_(r):
                for k in range(un):
                    body(r * un + k, k, r)
            if rounds:
                over(eng, 1, rounds, round_)
            for q in range(rounds * un, n_full):
                body(q, q % un, q // un)
            if TAILN:
                tail(n_full, n_full % un, n_full // un)

        def x_place(q, rows_):
            if isinstance(q, int) and q == NQF:
                return x_tail[0:rows_, :, :]
            return arena[0:rows_, bass.ds(q * XW, XW)].rearrange("p (b n) -> p b n", b=2)

        block = ctx.enter_context(nc.Block())

        @block.sync
        def _(sp):
            sp.dma_start(first_i, src[0:SLOTS * P].rearrange("(t e) -> t e", e=P)).then_inc(s_first, 16)
            if FULLB:
                for n, a in ((1, dst), (0, src)):
                    sp.dma_start(tab_i[n][:, 0:FULLB, :], a[0:FULLB * P * P].rearrange("(b p e) -> p b e", p=P, e=P)
                                 ).then_inc(s_tab[n], 16)
            sp.wait_ge(s_pad, 2)
            for n, a in ((1, dst), (0, src)):
                at = FULLB * P * P
                if RROWS:
                    sp.dma_start(tab_i[n][0:RROWS, FULLB, :], a[at:at + RROWS * P].rearrange("(p e) -> p e", e=P)
                                 ).then_inc(s_tab[n], 16)
                if REDGE:
                    at += RROWS * P
                    sp.dma_start(tab_i[n][RROWS:RROWS + 1, FULLB, 0:REDGE], a[at:E].rearrange("(p e) -> p e", p=1)
                                 ).then_inc(s_tab[n], 16)
            r = 0
            for a in (b1, g1, bt1, b2, g2, bt2):
                k = a.shape[0] // P
                sp.dma_start(prm[r:r + k, :], a.rearrange("(r c) -> r c", c=P)).then_inc(s_prm, 16)
                r += k
            sp.dma_start(eps1[:, :], eps_gin.partition_broadcast(P)).then_inc(s_prm, 16)
            sp.dma_start(W1s[:, :, :], W1.rearrange("(k p) n -> p k n", p=P)).then_inc(s_w, 16)
            sp.dma_start(W2s[:, :, :], W2.rearrange("(k p) n -> p k n", p=P)).then_inc(s_w, 16)

            def load_node_tile(c, n=P):
                if at_least(c, 1):
                    sp.wait_ge(s_hx, c)
                sp.dma_start(xt[0:n, :], x[bass.ds(c * P, n), :]).then_inc(s_xt, 16)

            def store_hT(c, b=0):
                sp.wait_ge(s_hTc, c + 1)
                sp.dma_start(t_dram[bass.ds(c, 1), :, FB * P:].rearrange("c p f -> (c p) f"),
                             hTs[b].rearrange("p f n -> p (f n)")).then_inc(s_hs, 16)

            def store_tT(c, b=0):
                sp.wait_ge(s_tb, c + 1)
                sp.dma_start(t_dram[bass.ds(c, 1), :, 0:FB * P].rearrange("c p f -> (c p) f"),
                             tb[b].rearrange("p f n -> p (f n)")).then_inc(s_td, 16)

            def node_tiles(c):
                load_node_tile(c + 1)
                store_hT(c)
                if at_least(c, 1):
                    store_tT(c - 1)
            load_node_tile(0)
            over(sp, 1, NT - 2, node_tiles)
            load_node_tile(NT - 1, LASTN)
            store_hT(NT - 2)
            store_tT(NT - 3)

            def load_t(q, k, r, tiles=Q):
                if at_least(q, 2):
                    sp.wait_ge(s_u, FB * (q - 1))
                of = t_dram[bass.ds(q * Q, tiles), :, :].rearrange("c p f -> p c f")
                sp.dma_start(tin[:, k % 2, 0:tiles, :, :].rearrange("p c f n -> p c (f n)"),
                             of[:, :, 0:FB * P]).then_inc(s_tin[k % 2], 16)
                if at_least(q, 2):
                    sp.wait_ge(s_y, q - 1)
                sp.dma_start(hin[:, k % 2, 0:tiles, :, :].rearrange("p c f n -> p c (f n)"),
                             of[:, :, FB * P:]).then_inc(s_hin[k % 2], 16)

            def load_x(q, rows_=P):
                k, r = q % XU, q // XU
                if r:
                    sp.wait_ge(s_x[k], 16 * r)
                sp.dma_start(x_place(q, rows_),
                             x[q * QN:q * QN + rows_ * 4, :].rearrange("(p b k) d -> p b (k d)", b=2, k=2)
                             ).then_inc(s_x[k], 16)
            sp.wait_ge(s_agg, GROUPS)
            sp.wait_ge(s_sel, GROUPS)
            sp.wait_ge(s_td, 16 * (NT - 2))
            sp.wait_ge(s_hs, 16 * (NT - 1))
            ahead = min(2, NQF - 1)
            for q in range(ahead):
                load_t(q, q, 0)
            store_hT(NT - 1, 1)
            store_tT(NT - 2)
            store_tT(NT - 1, 1)
            sp.wait_ge(s_td, 16 * NT)
            sp.wait_ge(s_hs, 16 * NT)
            sp.wait_ge(s_bn1, 5)

            def load_both(q, k, r):
                if at_least(q, ahead):
                    load_t(q, k, r)
                if isinstance(q, int) and q < 8:
                    for m in range(max(q, 2 * q - 2), min(max(q + 1, 2 * q), X_EARLY, NQF)):
                        load_x(m)
            chunks(sp, 8, NQF, load_both, lambda q, k, r: load_t(q, k, r, ceil(TAILN, P)))
            last = [NQ - 1 - (NQ - 1 - b) % 2 for b in (0, 1)]
            for m, s, v in ((20, s_u, FB * (last[1] + 1)),
                            (18, s_u, FB * (last[0] + 1)),
                            (16, s_c, last[1] + 1),
                            (14, s_c, last[0] + 1)):
                for q in range(m, min(m + 2, NQF)):
                    sp.wait_ge(s, v)
                    load_x(q)
            for q, b in ((23, 1), (22, 0)):
                if q < NQF:
                    sp.wait_ge(s_y, last[b] + 1)
                    load_x(q)
            if TAILN:
                sp.wait_ge(s_rl, DB)
                load_x(NQF, TAILN // 4)

        @block.gpsimd
        def _(pool):
            nc.gpsimd.memset(tab_i[0][:, EB - 1, :], 0).then_inc(s_pad, 1)
            nc.gpsimd.memset(tab_i[1][:, EB - 1, :], N).then_inc(s_pad, 1)
            nc.gpsimd.memset(ident[:, :], 0.0).then_inc(s_ident, 1)
            pool.wait_ge(s_ident, 1)
            nc.gpsimd.affine_select(out=ident[:, :], in_=ident[:, :], compare_op=ALU.not_equal, fill=1.0, base=0,
                                    pattern=[[-1, P]], channel_multiplier=1).then_inc(s_ident, 1)
            nc.gpsimd.iota(sched, pattern=[[P, NI], [0, GI]], base=P * (1 - LAG),
                           channel_multiplier=0).then_inc(s_iota, 1)
            nc.gpsimd.iota(iota_w[:, :], pattern=[[1, W]], base=0, channel_multiplier=0,
                           allow_small_or_imprecise_dtypes=True).then_inc(s_iota, 1)
            nc.gpsimd.memset(aggT[:, :, 0:ZP], 0.0).then_inc(s_zero, 1)

            def gather(i, groups=range(GI)):
                for j in groups:
                    g = i * GI + j
                    tiles = tiles_of(i, j)
                    if not tiles:
                        continue
                    if at_least(i, 1):
                        pool.wait_ge(s_h, g - GI + 1)
                    wait_apart(pool, s_idx, g + 1)
                    for k in range(tiles):
                        s = j * GT + k
                        nc.gpsimd.indirect_dma_start(
                            out=rows[:, s, :], out_offset=None, in_=x[:, :],
                            in_offset=bass.IndirectOffsetOnAxis(ap=idx[:, s:s + 1], axis=0)).then_inc(s_rows[j], 16)
            gather(0)
            gather(1, range(0, 2))
            pool.wait_ge(s_flag, 1)
            ok = pool.value_load(flag[0:1, 0:1], min_val=0, max_val=1)
            with pool.If(ok < 1):
                nc.gpsimd.iota(g_iota, pattern=[[1, GW]], base=0, channel_multiplier=0,
                               allow_small_or_imprecise_dtypes=True).then_inc(s_iota, 1)
                with pool.Fori(0, TILES) as t:
                    wait_apart(pool, s_gi, t + 1)
                    nc.gpsimd.indirect_dma_start(
                        out=g_row, out_offset=None, in_=x[:, :],
                        in_offset=bass.IndirectOffsetOnAxis(ap=g_idx, axis=0)).then_inc(s_gr, 16)
            gather(1, range(2, GI))
            with pool.Fori(2, NI - 1) as i:
                gather(i)
            gather(NI - 1)

            def store_out(q, k, r, rows_=P):
                pool.wait_ge(s_sum, q + 1)
                nc.gpsimd.dma_start(out[bass.ds(q * QN, rows_ * 4), :].rearrange("(p b k) d -> p b (k d)", b=2, k=2),
                                    x_place(q, rows_)).then_inc(s_o, 16)
            chunks(pool, XU, NQF, store_out, lambda q, k, r: store_out(q, k, r, TAILN // 4))
            pool.wait_ge(s_o, 16 * NQ)

        @block.vector
        def _(dve):
            V = nc.vector

            def partial_moments(rows_of, stats, s_stats):
                for r, o in zip(rows_of, stats):
                    last = V.bn_stats(o, r)
                last.then_inc(s_stats, 1)

            def moments(stats, mean_var, s_stats, s_mean, v):
                wait_apart(dve, s_stats, v)
                for o, m in zip(stats, mean_var):
                    last = V.bn_aggr(m, o)
                last.then_inc(s_mean, 1)

            def scale_and_shift(mean, std, shift, s_root, s_inv, s_done, v):
                dve.wait_ge(s_root, v)
                V.reciprocal(std, std).then_inc(s_inv, 1)
                dve.wait_ge(s_inv, v)
                V.scalar_tensor_tensor(shift, mean, -1.0, std, ALU.mult, ALU.mult).then_inc(s_done, 1)

            done = [0]

            def own(instruction):
                done[0] += 1
                instruction.then_inc(s_par, 1)
                dve.wait_ge(s_par, done[0])

            def zero_more(at, n):
                return V.tensor_copy(aggT[:, :, ZP + at * ZW:ZP + (at + n) * ZW], aggT[:, :, ZP:ZP + n * ZW])
            own(V.memset(row0, 0.0))
            own(V.memset(row0[0:1, :], 1.0))
            own(V.memset(aggT[:, :, ZP:ZP + ZW], 0.0))
            own(zero_more(1, 1))
            dve.wait_ge(s_first, 16)
            V.tensor_copy(first_f, first_i).then_inc(s_firstf, 1)
            dve.wait_ge(s_firstT, 1)
            V.tensor_copy(idx[:, :], misc_ps[:, 0:SLOTS]).then_inc(s_idx, GI)
            own(zero_more(2, 2))
            own(zero_more(4, 4))
            zero_more(8, 2)
            dve.wait_ge(s_tab[1], TAB_LOADS)
            V.tensor_copy(tab_f[1], tab_i[1]).then_inc(s_tabf[1], 1)
            zero_more(10, 2)
            for b in range(NTR):
                w = min(4, EB - 4 * b) * P
                dve.wait_ge(s_tr[1], b + 1)
                V.tensor_copy(dst_f[:, 4 * b * P:4 * b * P + w], tr_ps[1][b % 2][:, 0:w]).then_inc(s_trc[1], 1)

            def statistics(i, j):
                dve.wait_ge(s_rows[j], 64 * i + 16 * tiles_of(i, j))
                partial_moments([rows[:, j * GT + k, :] for k in range(GT)], [st[:, j % 2, k, :] for k in range(GT)],
                                s_bn)

            def mean_and_var(i, j):
                g, r = i * GI + j, j % 2
                if at_least(g, 2):
                    dve.wait_ge(s_h, g - 1)
                moments([st[:, r, k, :] for k in range(GT)], [mv[:, r, k, :] for k in range(GT)], s_bn, s_mv, g + 1)

            def scale(i, j):
                r = j % 2
                scale_and_shift(mv[:, r, :, 0], mv[:, r, :, 1], nb[:, r, :], s_sd, s_rstd, s_st, i * GI + j + 1)

            def selection(i, j):
                g = i * GI + j
                V.tensor_tensor(sel[:, j % 2, :, :],
                                rel[:, bass.ds(g * GT, GT)].unsqueeze(2).to_broadcast([P, GT, W]),
                                iota_w[:, :].unsqueeze(1).to_broadcast([P, GT, W]), ALU.is_equal).then_inc(s_sel, 1)

            def next_rows(i, j):
                V.tensor_copy(idx[:, j * GT:(j + 1) * GT],
                              src_i[:, bass.ds((i + 1) * SLOTS + j * GT, GT)]).then_inc(s_idx, 1)

            statistics(0, 0)
            mean_and_var(0, 0)
            dve.wait_ge(s_base, 1)
            own(V.tensor_scalar(base_f, misc_ps[:, 0:NG], HALF, None, ALU.add))
            dve.wait_ge(s_iota, 2)
            own(V.tensor_tensor(rel_g, dst_f[:, 0:NE].rearrange("p (g k) -> p g k", k=GT),
                                base_f.unsqueeze(2).to_broadcast([P, NG, GT]), ALU.subtract))
            scale(0, 0)
            dve.wait_ge(s_trc[0], NTR)
            next_rows(0, 0)
            own(V.tensor_scalar(iota_w[:, :], iota_w[:, :], -HALF, None, ALU.add))
            selection(0, 0)
            statistics(0, 1)
            mean_and_var(0, 1)
            own(V.tensor_tensor(base_f, base_f, sched, ALU.subtract))
            scale(0, 1)
            next_rows(0, 1)
            own(V.tensor_reduce(chk[:, 0:1], rel, X, ALU.max, apply_absolute_value=True))
            own(V.tensor_reduce(chk[:, 1:2], base_f, X, ALU.min))
            own(V.tensor_scalar(chk[:, 2:3], chk[:, 0:1], -1.0, 2 * HALF, ALU.mult, ALU.add))
            V.tensor_reduce(chk[:, 3:4], chk[:, 1:3], X, ALU.min).then_inc(s_pre, 1)
            selection(0, 1)
            V.tensor_copy(base_i[:, :], misc_ps[0:1, 0:NG]).then_inc(s_pre, 1)
            dve.wait_ge(s_flagT, 2)
            own(V.tensor_reduce(flag_f[:, :], flag_ps, X, ALU.min))
            V.tensor_scalar(flag[:, :], flag_f[:, :], HALF, None, ALU.is_ge).then_inc(s_flag, 1)
            V.tensor_copy(prmT[:, :], prm_ps).then_inc(s_par, 1)
            V.tensor_scalar(eps1[:, :], eps1[:, :], 1.0, None, ALU.add).then_inc(s_par, 1)
            zero_more(12, 4).then_inc(s_zero, 1)
            dve.wait_ge(s_par, done[0] + 2)
            dve.wait_ge(s_flag, 1)
            ok = dve.value_load(flag[0:1, 0:1], min_val=0, max_val=1)
            dve.wait_ge(s_zero, 4)
            dve.wait_ge(s_pre, 2)

            with dve.If(ok < 1):
                dve.wait_ge(s_iota, 3)
                V.memset(g_nb, 0.0).then_inc(s_gd, 1)
                with dve.Fori(0, TILES) as t:
                    own = t * (4 + 2 * NW) + 1
                    dve.wait_ge(s_gd, own)
                    V.tensor_copy(g_idx, src_i[:, bass.ds(t, 1)]).then_inc(s_gi, 1)
                    V.tensor_copy(g_dst, dst_f[:, bass.ds(t, 1)]).then_inc(s_gd, 1)
                    dve.wait_ge(s_gr, 16 * t + 16)
                    V.bn_stats(g_stat, g_row).then_inc(s_gd, 1)
                    wait_apart(dve, s_gd, own + 2)
                    V.bn_aggr(g_mv, g_stat).then_inc(s_gv, 1)
                    dve.wait_ge(s_gq, t + 1)
                    V.reciprocal(g_mv[:, 1:2], g_mv[:, 1:2]).then_inc(s_gd, 1)
                    dve.wait_ge(s_gd, own + 3)
                    V.scalar_tensor_tensor(g_nb, g_mv[:, 0:1], -1.0, g_mv[:, 1:2], ALU.mult, ALU.mult).then_inc(s_gs, 1)
                    dve.wait_ge(s_gh, t + 1)
                    V.memset(g_nb, 0.0).then_inc(s_gd, 1)
                    with dve.Fori(0, NW) as w:
                        n = t * NW + w
                        dve.wait_ge(s_gd, own + 4 + 2 * w)
                        V.tensor_tensor(g_sel, g_iota, g_dst.to_broadcast([P, GW]), ALU.is_equal).then_inc(s_gm, 1)
                        dve.wait_ge(s_gm, n + 1)
                        V.tensor_scalar(g_dst, g_dst, float(-GW), None, ALU.add).then_inc(s_gd, 1)
                        dve.wait_ge(s_gp, n + 1)
                        z = aggT[:, :, bass.ds(w * GW, GW)]
                        V.tensor_tensor(z, z, g_ps[:, :, 0:GW], ALU.add).then_inc(s_gd, 1)
                V.memset(base_i[:, :], NT * P).then_inc(s_gend, 1)
                dve.wait_ge(s_gend, 1)
                dve.wait_ge(s_gd, TILES * (4 + 2 * NW) + 1)

            def add_window(g, r):
                at = dve.value_load(base_i[0:1, bass.ds(g, 1)], min_val=0, max_val=NT * P)
                dve.wait_ge(s_agg, g + 1)
                if at_least(g, 1):
                    dve.wait_ge(s_add, g)
                z = aggT[:, :, bass.ds(at, W)]
                V.tensor_tensor(z, z, agg_ps[r], ALU.add).then_inc(s_add, 1)

            def statistics_node_tile(c, n=P):
                dve.wait_ge(s_xt, 16 * c + 16)
                partial_moments([xt[0:n, :]], [xst[0:n, :]], s_xbn)

            def mean_and_var_node_tile(c, n=P):
                moments([xst[0:n, :]], [xmv[0:n, :]], s_xbn, s_xmv, c + 1)

            def scale_node_tile(c, n=P):
                scale_and_shift(xmv[0:n, 0:1], xmv[0:n, 1:2], xnb[0:n, :], s_xsd, s_xrs, s_xst, c + 1)

            def z_tile(c, added, n=P, b=0):
                dve.wait_ge(s_hTc, c + 1)
                dve.wait_ge(s_add, added)
                if at_least(c, 1) and b == 0:
                    dve.wait_ge(s_t, c)
                V.scalar_tensor_tensor(zt[b][:, :, 0:n], hTs[b][:, :, 0:n], eps1[:, 0:1], aggT[:, :, bass.ds(c * P, n)],
                                       ALU.mult, ALU.add).then_inc(s_zt, 1)

            def t_stats(c, n=P, b=0):
                dve.wait_ge(s_tb, c + 1)
                for f in range(FB):
                    last = V.bn_stats(st1[:, f, bass.ds(c * 6, 6)], tb[b][:, f, 0:n])
                last.then_inc(s_tst, 1)

            def iteration(i):
                a, c = i - LAG + 1, i - LAG
                for j in range(GI):
                    if not tiles_of(i, j):
                        continue
                    if not at_least(i * GI + j, 2):
                        continue
                    statistics(i, j)
                    if at_least(a, 0) and j == 0:
                        statistics_node_tile(a)
                    add_window(i * GI + j - 2, j % 2)
                    mean_and_var(i, j)
                    if at_least(a, 0) and j == 0:
                        mean_and_var_node_tile(a)
                    selection(i, j)
                    if not isinstance(i, int) or i < NI - 1:
                        next_rows(i, j)
                    if at_least(c, 1) and j == 1:
                        t_stats(c - 1)
                    scale(i, j)
                    if at_least(a, 0) and j == 0:
                        scale_node_tile(a)
                    if at_least(c, 0) and j == 1:
                        z_tile(c, i * GI)
            over(dve, LAG + 1, NI - 1, iteration)
            iteration(NI - 1)
            statistics_node_tile(NT - 1, LASTN)
            mean_and_var_node_tile(NT - 1, LASTN)
            V.memset(tb[1], 0.0)
            add_window(GROUPS - 2, GROUPS % 2)
            scale_node_tile(NT - 1, LASTN)
            add_window(GROUPS - 1, (GROUPS - 1) % 2)
            z_tile(NT - 2, GROUPS)
            t_stats(NT - 3)
            z_tile(NT - 1, GROUPS, LASTN, 1)
            t_stats(NT - 2)
            t_stats(NT - 1, LASTN, 1)

            def batch_norm(stats_, mean_var, gT, btT, scale, shift, tmp, blocks, s_own, s_root, s_stats, v):
                dve.wait_ge(s_stats, v)
                for f in range(blocks):
                    last = V.bn_aggr(mean_var[:, f, :], stats_[:, f, :])
                last.then_inc(s_own, 1)
                dve.wait_ge(s_root, 1)
                V.reciprocal(tmp[:, :], tmp[:, :]).then_inc(s_own, 1)
                dve.wait_ge(s_own, 2)
                V.tensor_tensor(scale[:, :], tmp[:, :], gT, ALU.mult).then_inc(s_own, 1)
                dve.wait_ge(s_own, 3)
                V.tensor_tensor(tmp[:, :], mean_var[:, :, 0], scale[:, :], ALU.mult).then_inc(s_own, 1)
                dve.wait_ge(s_own, 4)
                V.tensor_tensor(shift[:, :], btT, tmp[:, :], ALU.subtract).then_inc(s_own, 1)
            batch_norm(st1, mv1, g1T, bt1T, sc1, sh1, tmp1, FB, s_bn1, s_root1, s_tst, NT)

            def y_chunk(q, k, r, n=QN):
                dve.wait_ge(s_hin[k % 2], 32 * r + 16 * (k // 2) + 16)
                dve.wait_ge(s_c, q + 1)
                tiles = ceil(n, P)
                for f in range(DB):
                    for a, b, t0, t1 in (((0, n, 0, tiles),) if n % P == 0 else
                                         ((0, n - n % P, 0, tiles - 1), (n - n % P, n, tiles - 1, tiles))):
                        if a == b:
                            continue
                        w = min(P, b - a)
                        last = V.scalar_tensor_tensor(
                            aggT[:, f, bass.ds(q * QN + a, b - a)].rearrange("p (c n) -> p c n", n=w),
                            c_ps[k % 2][f][:, a:b].rearrange("p (c n) -> p c n", n=w), b2T[:, f:f + 1],
                            hin[:, k % 2, t0:t1, f, 0:w], ALU.add, ALU.add)
                last.then_inc(s_y, 1)
                dve.wait_ge(s_y, q + 1)
                for f in range(DB):
                    last = V.bn_stats(st2[:, f, bass.ds(q * 6, 6)], aggT[:, f, bass.ds(q * QN, n)])
                last.then_inc(s_yst, 1)
            chunks(dve, 4, NQF, y_chunk, lambda q, k, r: y_chunk(q, k, r, TAILN))
            batch_norm(st2, mv2, g2T, bt2T, sc2, sh2, tmp2, DB, s_bn2, s_root2, s_yst, NQ)

            def residual(q, k, r, rows_=P):
                dve.wait_ge(s_x[k], 16 * r + 16)
                dve.wait_ge(s_oT, q + 1)
                V.tensor_tensor(x_place(q, rows_), o_ps[k % 2][0:rows_, :, :],
                                x_place(q, rows_), ALU.add).then_inc(s_sum, 1)
            chunks(dve, XU, NQF, residual, lambda q, k, r: residual(q, k, r, TAILN // 4))

        @block.scalar
        def _(act):
            S = nc.scalar
            act.preload_act_table(ACT.Sqrt)

            def zero_step(n):
                S.memzero(aggT[:, :, ZA[n]:ZA[n + 1]]).then_inc(s_zero, 1)
            zero_step(0)
            act.wait_ge(s_tab[0], TAB_LOADS)
            S.copy(tab_f[0], tab_i[0]).then_inc(s_tabf[0], 1)
            for b in range(NTR):
                w = min(4, EB - 4 * b) * P
                act.wait_ge(s_tr[0], b + 1)
                S.copy(src_i[:, 4 * b * P:4 * b * P + w], tr_ps[0][b % 2][:, 0:w]).then_inc(s_trc[0], 1)

            def root(i, j):
                act.wait_ge(s_mv, i * GI + j + 1)
                var = mv[:, j % 2, :, 1]
                S.activation(var, var, ACT.Sqrt, bias=LN_EPS).then_inc(s_sd, 1)

            def root_node_tile(c, n=P):
                act.wait_ge(s_xmv, c + 1)
                S.activation(xmv[0:n, 1:2], xmv[0:n, 1:2], ACT.Sqrt, bias=LN_EPS).then_inc(s_xsd, 1)

            def normalise(i, j):
                g, r = i * GI + j, j % 2
                act.wait_ge(s_st, g + 1)
                if at_least(g, 2):
                    act.wait_ge(s_agg, g - 1)
                for k in range(GT):
                    last = S.activation(hrow[:, r, k, :], rows[:, j * GT + k, :], ACT.Relu,
                                        bias=nb[:, r, k:k + 1], scale=mv[:, r, k, 1:2])
                last.then_inc(s_h, 1)

            def norm_node_tile(c, n=P):
                act.wait_ge(s_xst, c + 1)
                if at_least(c, 1):
                    act.wait_ge(s_hT, c)
                S.activation(hx[0:n, :], xt[0:n, :], ACT.Relu, bias=xnb[0:n, :], scale=xmv[0:n, 1:2]).then_inc(s_hx, 1)

            def copy_hT(c, n=P, b=0):
                act.wait_ge(s_hT, c + 1)
                if at_least(c, 1) and b == 0:
                    act.wait_ge(s_hs, 16 * c)
                    act.wait_ge(s_zt, c)
                S.copy(hTs[b][:, :, 0:n], hT_ps[:, :, 0:n]).then_inc(s_hTc, 1)

            def t_and_b1(c, n=P, b=0):
                act.wait_ge(s_t, c + 1)
                if at_least(c, 1) and b == 0:
                    act.wait_ge(s_td, 16 * c)
                    act.wait_ge(s_tst, c)
                for f in range(FB):
                    last = S.activation(tb[b][:, f, 0:n], t_ps[b][:, f, 0:n], ACT.Identity, bias=b1T[:, f:f + 1],
                                        scale=1.0)
                last.then_inc(s_tb, 1)

            for j in range(2):
                root(0, j)
                normalise(0, j)
            zero_step(1)
            act.wait_ge(s_flag, 1)
            ok = act.value_load(flag[0:1, 0:1], min_val=0, max_val=1)
            with act.If(ok < 1):
                with act.Fori(0, TILES) as t:
                    act.wait_ge(s_gv, t + 1)
                    S.activation(g_mv[:, 1:2], g_mv[:, 1:2], ACT.Sqrt, bias=LN_EPS).then_inc(s_gq, 1)
                    act.wait_ge(s_gs, t + 1)
                    S.activation(g_h, g_row, ACT.Relu, bias=g_nb, scale=g_mv[:, 1:2]).then_inc(s_gh, 1)
                act.wait_ge(s_gend, 1)

            def iteration(i):
                a, c = i - LAG + 1, i - LAG
                for j in range(GI):
                    if not tiles_of(i, j) or not at_least(i * GI + j, 2):
                        continue
                    root(i, j)
                    if at_least(a, 0) and j == 0:
                        root_node_tile(a)
                    normalise(i, j)
                    if at_least(a, 0) and j == 0:
                        norm_node_tile(a)
                    if at_least(a, 0) and j == 2:
                        copy_hT(a)
                if isinstance(i, int) and i == NI - 1:
                    root_node_tile(NT - 1, LASTN)
                    norm_node_tile(NT - 1, LASTN)
                if at_least(c, 0):
                    t_and_b1(c)
            over(act, LAG + 1, NI - 1, iteration)
            iteration(NI - 1)
            copy_hT(NT - 1, LASTN, 1)
            t_and_b1(NT - 2)
            t_and_b1(NT - 1, LASTN, 1)

            def batch_root(mean_var, tmp, s_own, s_root):
                act.wait_ge(s_own, 1)
                S.activation(tmp[:, :], mean_var[:, :, 1], ACT.Sqrt, bias=BN_EPS).then_inc(s_root, 1)
            batch_root(mv1, tmp1, s_bn1, s_root1)
            act.wait_ge(s_bn1, 5)

            def relu1(q, k, r, tiles=Q):
                act.wait_ge(s_tin[k % 2], 32 * r + 16 * (k // 2) + 16)
                if at_least(q, 2):
                    act.wait_ge(s_c, q - 1)
                for f in range(FB):
                    S.activation(u[:, k % 2, f, 0:tiles * P].rearrange("p (c n) -> p c n", n=P),
                                 tin[:, k % 2, 0:tiles, f, :], ACT.Relu, bias=sh1[:, f:f + 1],
                                 scale=sc1[:, f:f + 1]).then_inc(s_u, 1)
            chunks(act, 4, NQF, relu1, lambda q, k, r: relu1(q, k, r, ceil(TAILN, P)))
            batch_root(mv2, tmp2, s_bn2, s_root2)
            act.wait_ge(s_bn2, 5)

            def relu2(q, k, r, n=QN):
                if at_least(q, 2):
                    act.wait_ge(s_oT, q - 1)
                for f in range(DB):
                    S.activation(rl[k % 2][:, f, 0:n], aggT[:, f, bass.ds(q * QN, n)], ACT.Relu,
                                 bias=sh2[:, f:f + 1], scale=sc2[:, f:f + 1]).then_inc(s_rl, 1)
            chunks(act, XU, NQF, relu2, lambda q, k, r: relu2(q, k, r, TAILN))

        @block.tensor
        def _(pe):
            T = nc.tensor
            pe.wait_ge(s_ident, 2)
            pe.wait_ge(s_firstf, 1)
            T.transpose(misc_ps[:, 0:SLOTS], first_f, ident[0:SLOTS, 0:SLOTS]).then_inc(s_firstT, 1)

            def table(n, banks):
                pe.wait_ge(s_tabf[n], 1)
                for b in banks:
                    if b >= 2:
                        pe.wait_ge(s_trc[n], b - 1)
                    for m in range(min(4, EB - 4 * b)):
                        last = T.transpose(tr_ps[n][b % 2][:, m * P:(m + 1) * P], tab_f[n][:, 4 * b + m, :],
                                           ident[:, :])
                    last.then_inc(s_tr[n], 1)
            table(1, range(NTR))
            table(0, range(1))
            pe.wait_ge(s_trc[1], NTR)
            pe.wait_ge(s_par, 2)
            T.matmul(misc_ps[:, 0:NG], row0, dst_f[:, 0:NE:GT], start=True, stop=True).then_inc(s_base, 1)
            table(0, range(1, NTR))

            def aggregate(i, j):
                g, r = i * GI + j, j % 2
                pe.wait_ge(s_h, g + 1)
                pe.wait_ge(s_sel, g + 1)
                if at_least(g, 2):
                    pe.wait_ge(s_add, g - 1)
                for f in range(DB):
                    for k in range(GT):
                        last = T.matmul(agg_ps[r][:, f, :], hrow[:, r, k, f * P:(f + 1) * P], sel[:, r, k, :],
                                        start=k == 0, stop=k == GT - 1)
                last.then_inc(s_agg, 1)

            def transpose_h(c, n=P):
                pe.wait_ge(s_hx, c + 1)
                if at_least(c, 1):
                    pe.wait_ge(s_hTc, c)
                for f in range(DB):
                    last = T.transpose(hT_ps[:, f, 0:n], hx[0:n, f * P:(f + 1) * P], ident[0:n, 0:n])
                last.then_inc(s_hT, 1)

            def times_W1(c, n=P, b=0):
                pe.wait_ge(s_zt, c + 1)
                if at_least(c, 1) and b == 0:
                    pe.wait_ge(s_tb, c)
                for m in range(FB):
                    for k in range(DB):
                        last = T.matmul(t_ps[b][:, m, 0:n], W1s[:, k, m * P:(m + 1) * P], zt[b][:, k, 0:n],
                                        start=k == 0, stop=k == DB - 1)
                last.then_inc(s_t, 1)

            aggregate(0, 0)
            pe.wait_ge(s_prm, 16 * 7)
            T.transpose(prm_ps, prm[:, :], ident[0:18, 0:18]).then_inc(s_flagT, 1)
            pe.wait_ge(s_pre, 1)
            T.transpose(flag_ps, chk[:, 3:4], ident[:, :]).then_inc(s_flagT, 1)
            aggregate(0, 1)
            pe.wait_ge(s_flag, 1)
            ok = pe.value_load(flag[0:1, 0:1], min_val=0, max_val=1)
            with pe.If(ok < 1):
                with pe.Fori(0, TILES) as t:
                    wait_apart(pe, s_gh, t + 1)
                    with pe.Fori(0, NW) as w:
                        pe.wait_ge(s_gm, t * NW + w + 1)
                        for f in range(DB):
                            last = T.matmul(g_ps[:, f, 0:GW], g_h[:, f * P:(f + 1) * P], g_sel, start=True, stop=True)
                        last.then_inc(s_gp, 1)
                pe.wait_ge(s_gend, 1)

            def iteration(i):
                a, c = i - LAG + 1, i - LAG
                for j in range(GI):
                    if not tiles_of(i, j) or not at_least(i * GI + j, 2):
                        continue
                    last = isinstance(i, int) and i == NI - 1
                    if last and j == 1:
                        times_W1(c)
                    aggregate(i, j)
                    if at_least(a, 0) and j == 0:
                        transpose_h(a)
                    if at_least(c, 0) and j == 1 and not last:
                        times_W1(c)
            pe.wait_ge(s_w, 32)
            over(pe, LAG + 1, NI - 1, iteration)
            iteration(NI - 1)
            transpose_h(NT - 1, LASTN)
            times_W1(NT - 2)
            times_W1(NT - 1, LASTN, 1)

            def times_W2(q, k, r, n=QN):
                if at_least(q, 2):
                    pe.wait_ge(s_y, q - 1)
                for m in range(DB):
                    for f in range(FB):
                        if m == 0:
                            pe.wait_ge(s_u, FB * q + f + 1)
                        last = T.matmul(c_ps[k % 2][m][:, 0:n], W2s[:, f, m * P:(m + 1) * P], u[:, k % 2, f, 0:n],
                                        start=f == 0, stop=f == FB - 1)
                last.then_inc(s_c, 1)
            chunks(pe, 4, NQF, times_W2, lambda q, k, r: times_W2(q, k, r, TAILN))

            def transpose_out(q, k, r, n=QN):
                if at_least(q, 2):
                    pe.wait_ge(s_sum, q - 1)
                for f in range(DB):
                    pe.wait_ge(s_rl, DB * q + f + 1)
                    for m in range(4):
                        at = (m % 2) * D + f * P
                        last = T.transpose(o_ps[k % 2][0:n // 4, m // 2, at:at + P],
                                           rl[k % 2][:, f, m:n:4], ident[:, :])
                last.then_inc(s_oT, 1)
            chunks(pe, XU, NQF, transpose_out, lambda q, k, r: transpose_out(q, k, r, TAILN))


_INS = ["x", "src", "dst", "L0_gnn_W1", "L0_gnn_b1", "L0_gnn_g1", "L0_gnn_bt1", "L0_gnn_W2", "L0_gnn_b2",
        "L0_gnn_g2", "L0_gnn_bt2", "L0_gnn_eps_gin"]


def kernel(**inputs):
    import numpy as np
    import concourse.bacc as bacc
    from concourse.bass_utils import run_bass_kernel_spmd

    nc = bacc.Bacc("TRN2", target_bir_lowering=False, num_devices=1)
    arrays, args = {}, []
    for name in _INS:
        a = np.ascontiguousarray(inputs[name])
        if name.endswith("eps_gin"):
            a = a.reshape(1, 1)
        arrays[f"in_{name}"] = a
        args.append(nc.dram_tensor(f"in_{name}", a.shape, mybir.dt.from_np(a.dtype), kind="ExternalInput").ap())
    out = nc.dram_tensor("out", inputs["x"].shape, mybir.dt.float32, kind="ExternalOutput").ap()
    build(nc, *args, out)
    r = run_bass_kernel_spmd(nc, [arrays], core_ids=[0])
    return r.results[0]["out"]
```

```python
import concourse.bass as bass
from concourse import mybir
from contextlib import ExitStack

P = 128
D = 256
F = 512
DB, FB = D // P, F // P
GT = 4
GI = 4
SLOTS = GT * GI
W = 96
HALF = (W - 1) / 2
LN_EPS = BN_EPS = 1e-5
BANK = 512
Q = 4
QN = Q * P
XU = 8
XW = Q * D
X_FIRST = 7
X_EARLY = 16


def ceil(a, b):
    return -(-a // b)


def build(nc, x, src, dst, W1, b1, g1, bt1, W2, b2, g2, bt2, eps_gin, out):
    f32, i32 = mybir.dt.float32, mybir.dt.int32
    ALU = mybir.AluOpType
    ACT = mybir.ActivationFunctionType
    X = mybir.AxisListType.X
    N, E = x.shape[0], src.shape[0]

    NI = ceil(E, P * SLOTS)
    NT = ceil(N, P)
    assert NI == NT and NI >= 4 and N % 4 == 0 and NI * GI <= BANK
    LASTN = N - P * (NT - 1)
    NG, NE = NI * GI, NI * SLOTS
    TILES = ceil(E, P)
    GROUPS = ceil(TILES, GT)
    EB = ceil(NE, P)
    FULLB = E // (P * P)
    RROWS = E // P - FULLB * P
    REDGE = E % P
    NZ = NT * P + W
    GW = max(w for w in range(1, BANK + 1) if N % w == 0)
    NW = N // GW
    LAG = 2
    NQF, NQ = N // QN, ceil(N, QN)
    TAILN = N - NQF * QN

    ctx = ExitStack()
    with ctx:
        def sb(name, shape, dt=f32):
            return ctx.enter_context(nc.sbuf_tensor(name, shape, dt))

        def sem(name):
            return ctx.enter_context(nc.semaphore(name))

        t_dram = nc.dram_tensor("t_T", (NT, P, FB * P), f32, kind="Internal").ap()

        aggT = sb("aggT", [P, DB, NZ])
        n_st1, n_w1, n_sel, n_tb, n_zt = max(FB * NT * 6, 512 + 2 * NG), DB * F, 2 * GT * W, FB * P, DB * P
        ONCE = [n_st1, n_w1, n_sel, n_tb, n_zt, D, D]
        MAIN = [8192, sum(ONCE), 2 * EB * P + NE, (SLOTS + 2 * GT) * D]
        U_AT = X_EARLY * XW
        TIN_AT = U_AT + 2 * FB * QN
        ST2_AT = TIN_AT + 2 * Q * FB * P
        assert TIN_AT >= sum(MAIN[:2])
        assert NQF * XW <= ST2_AT
        arena = sb("arena", [P, max(sum(MAIN), ST2_AT + DB * NQ * 6)])
        work, once, tables, ring = (arena[:, sum(MAIN[:n]):sum(MAIN[:n + 1])] for n in range(4))
        LAST_AT = X_FIRST * XW
        assert LAST_AT >= 4 * EB * P and LAST_AT + DB * P + FB * P <= 8192
        u = arena[:, U_AT:TIN_AT].rearrange("p (b f n) -> p b f n", b=2, n=QN)
        tin = arena[:, TIN_AT:ST2_AT].rearrange("p (b c f n) -> p b c f n", b=2, c=Q, n=P)
        st2 = arena[:, ST2_AT:ST2_AT + DB * NQ * 6].rearrange("p (f s) -> p f s", f=DB)
        rows = ring[:, 0:SLOTS * D].rearrange("p (s d) -> p s d", d=D)
        hrow = ring[:, SLOTS * D:].rearrange("p (b s d) -> p b s d", b=2, d=D)
        tab_i = [work[:, n * EB * P:(n + 1) * EB * P].bitcast(i32).rearrange("p (b e) -> p b e", e=P) for n in (0, 1)]
        tab_f = [work[:, (2 + n) * EB * P:(3 + n) * EB * P].rearrange("p (b e) -> p b e", e=P) for n in (0, 1)]
        piece = [once[:, sum(ONCE[:n]):sum(ONCE[:n + 1])] for n in range(len(ONCE))]
        g_row, g_h = work[:, 0:D], work[:, D:2 * D]
        g_sel = work[:, 2 * D:2 * D + GW]
        g_iota = work[:, 1024:1024 + GW]
        g_dst = work[:, 1600:1601]
        g_stat, g_mv, g_nb = work[:, 1610:1616], work[:, 1620:1622], work[:, 1624:1625]
        g_idx = work[:, 1632:1633].bitcast(i32)
        src_i = tables[:, 0:EB * P].bitcast(i32)
        dst_f = tables[:, EB * P:2 * EB * P]
        rel = tables[:, 2 * EB * P:2 * EB * P + NE]
        rel_g = rel.rearrange("p (g k) -> p g k", k=GT)
        idx = sb("idx", [P, SLOTS], i32)
        base_i = sb("base_i", [1, NG], i32)
        sel = piece[2].rearrange("p (b k w) -> p b k w", b=2, w=W)
        early_ = piece[0]
        first_i = early_[0:SLOTS, 0:P].bitcast(i32)
        first_f = early_[0:SLOTS, P:2 * P]
        row0 = early_[:, 2 * P:3 * P]
        base_f = early_[:, 384:384 + NG]
        sched = early_[:, 384 + NG:384 + 2 * NG].bitcast(i32)
        iota_w = sb("iota_w", [P, W])
        ident = sb("ident", [P, P])
        prm = early_[0:18, 384 + 2 * NG:384 + 2 * NG + P]
        prmT = sb("prmT", [P, 18])
        b1T, g1T, bt1T = prmT[:, 0:4], prmT[:, 4:8], prmT[:, 8:12]
        b2T, g2T, bt2T = prmT[:, 12:14], prmT[:, 14:16], prmT[:, 16:18]
        eps1 = sb("eps1", [P, 1])
        chk = sb("chk", [P, 4])
        flag_f = sb("flag_f", [1, 1])
        flag = sb("flag", [1, 1], i32)
        st = sb("st", [P, 2, GT, 6])
        mv = sb("mv", [P, 2, GT, 2])
        nb = sb("nb", [P, 2, GT])
        xt = piece[5]
        xst = sb("xst", [P, 6])
        xmv = sb("xmv", [P, 2])
        xnb = sb("xnb", [P, 1])
        hx = piece[6]
        zt = [a.rearrange("p (f n) -> p f n", n=P) for a in (piece[4], work[:, LAST_AT:LAST_AT + n_zt])]
        tb = [a.rearrange("p (f n) -> p f n", n=P) for a in
              (piece[3], work[:, LAST_AT + n_zt:LAST_AT + n_zt + n_tb])]
        W1s = piece[1].rearrange("p (k n) -> p k n", n=F)
        W2s = sb("W2s", [P, FB, D])
        st1 = piece[0][:, 0:FB * NT * 6].rearrange("p (f s) -> p f s", f=FB)
        x_tail = aggT[:, :, 0:QN]
        rl = [W2s.rearrange("p f d -> p (f d)").rearrange("p (f n) -> p f n", n=QN),
              sb("rl_odd", [P, DB, QN])]
        mv1 = sb("mv1", [P, FB, 2])
        sc1 = sb("sc1", [P, FB])
        sh1 = sb("sh1", [P, FB])
        tmp1 = sb("tmp1", [P, FB])
        mv2 = sb("mv2", [P, DB, 2])
        sc2 = sb("sc2", [P, DB])
        sh2 = sb("sh2", [P, DB])
        tmp2 = sb("tmp2", [P, DB])

        ps = ctx.enter_context(nc.psum_tensor("ps", [P, 8, BANK], f32))
        agg_ps = [ps[:, b, 0:DB * W].rearrange("p (f w) -> p f w", w=W) for b in (0, 1)]
        hT_ps = [ps[:, b, 0:D].rearrange("p (f n) -> p f n", n=P) for b in (2, 5, 6)]
        t_ps = [ps[:, b, :].rearrange("p (f n) -> p f n", n=P) for b in (3, 4)]
        tr_ps = [[ps[:, 2 + b, :] for b in (0, 1)], [ps[:, 4 + b, :] for b in (0, 1)]]
        misc_ps = ps[:, 6, :]
        prm_ps = ps[:, 7, 0:18]
        flag_ps = ps[0:1, 5, 0:P]
        g_ps = ps[:, 6:8, :]
        c_ps = [[ps[:, 2 * b + f, :] for f in range(DB)] for b in (0, 1)]
        o_ps = [ps[:, 4 + 2 * b:6 + 2 * b, :] for b in (0, 1)]

        s_ident, s_iota, s_pad, s_zero, s_w = (sem(n) for n in ("s_ident", "s_iota", "s_pad", "s_zero", "s_w"))
        s_apart = sem("s_apart")
        s_first, s_firstf, s_firstT = sem("s_first"), sem("s_firstf"), sem("s_firstT")
        s_tab = [sem("s_tab_src"), sem("s_tab_dst")]
        s_prm, s_par = sem("s_prm"), sem("s_par")
        s_tabf, s_tr, s_trc = ([sem(f"{a}_{b}") for b in ("src", "dst")] for a in ("s_tabf", "s_tr", "s_trc"))
        s_base, s_pre, s_flagT, s_flag = sem("s_base"), sem("s_pre"), sem("s_flagT"), sem("s_flag")
        s_gd, s_gi, s_gr, s_gs, s_gh, s_gm, s_gp, s_gv, s_gq, s_gend = (
            sem(n) for n in ("s_gd", "s_gi", "s_gr", "s_gs", "s_gh", "s_gm", "s_gp", "s_gv", "s_gq", "s_gend"))
        s_idx = sem("s_idx")
        s_rows = [sem(f"s_rows{j}") for j in range(GI)]
        s_bn, s_mv, s_sd, s_rstd, s_st, s_h, s_sel, s_agg, s_add = (
            sem(n) for n in ("s_bn", "s_mv", "s_sd", "s_rstd", "s_st", "s_h", "s_sel", "s_agg", "s_add"))
        s_xt, s_xbn, s_xmv, s_xsd, s_xrs, s_xst, s_hx, s_hT, s_hTc, s_zt, s_t, s_tb, s_tst, s_td = (
            sem(n) for n in ("s_xt", "s_xbn", "s_xmv", "s_xsd", "s_xrs", "s_xst", "s_hx", "s_hT", "s_hTc", "s_zt",
                             "s_t", "s_tb", "s_tst", "s_td"))
        s_bn1, s_bn2, s_root1, s_root2 = sem("s_bn1"), sem("s_bn2"), sem("s_root1"), sem("s_root2")
        s_tin = [sem(f"s_tin{b}") for b in range(2)]
        s_u, s_c, s_y, s_yst = sem("s_u"), sem("s_c"), sem("s_y"), sem("s_yst")
        s_x = [sem(f"s_x{b}") for b in range(XU)]
        s_o = sem("s_o")
        s_rl, s_oT, s_sum = sem("s_rl"), sem("s_oT"), sem("s_sum")

        NTR = ceil(EB, 4)
        ZP, ZW = NZ // 24, NZ // 32
        ZV = ZP + 12 * ZW
        ZA = [ZV, ZV + NZ // 4, ZV + NZ * 5 // 12, NZ]

        def wait_apart(eng, s, value):
            eng.wait_ge(s, value)
            eng.sem_inc(s_apart, 1)

        def tiles_of(i, j):
            return GT if not isinstance(i, int) or i < NI - 1 else max(0, min(GT, TILES - (i * GI + j) * GT))

        TAB_LOADS = 16 * (bool(FULLB) + bool(RROWS) + bool(REDGE))

        def at_least(i, least):
            return not isinstance(i, int) or i >= least

        def over(eng, first, n, body):
            for i in range(min(first, n)):
                body(i)
            if n > first:
                with eng.Fori(first, n) as i:
                    body(i)

        def chunks(eng, un, n_full, body, tail):
            rounds = n_full // un

            def round_(r):
                for k in range(un):
                    body(r * un + k, k, r)
            if rounds:
                over(eng, 1, rounds, round_)
            for q in range(rounds * un, n_full):
                body(q, q % un, q // un)
            if TAILN:
                tail(n_full, n_full % un, n_full // un)

        def x_place(q, rows_):
            if isinstance(q, int) and q == NQF:
                return x_tail[0:rows_, :, :]
            return arena[0:rows_, bass.ds(q * XW, XW)].rearrange("p (b n) -> p b n", b=2)

        block = ctx.enter_context(nc.Block())

        @block.sync
        def _(sp):
            sp.dma_start(first_i, src[0:SLOTS * P].rearrange("(t e) -> t e", e=P)).then_inc(s_first, 16)
            if FULLB:
                for n, a in ((1, dst), (0, src)):
                    sp.dma_start(tab_i[n][:, 0:FULLB, :], a[0:FULLB * P * P].rearrange("(b p e) -> p b e", p=P, e=P)
                                 ).then_inc(s_tab[n], 16)
            sp.wait_ge(s_pad, 2)
            for n, a in ((1, dst), (0, src)):
                at = FULLB * P * P
                if RROWS:
                    sp.dma_start(tab_i[n][0:RROWS, FULLB, :], a[at:at + RROWS * P].rearrange("(p e) -> p e", e=P)
                                 ).then_inc(s_tab[n], 16)
                if REDGE:
                    at += RROWS * P
                    sp.dma_start(tab_i[n][RROWS:RROWS + 1, FULLB, 0:REDGE], a[at:E].rearrange("(p e) -> p e", p=1)
                                 ).then_inc(s_tab[n], 16)
            r = 0
            for a in (b1, g1, bt1, b2, g2, bt2):
                k = a.shape[0] // P
                sp.dma_start(prm[r:r + k, :], a.rearrange("(r c) -> r c", c=P)).then_inc(s_prm, 16)
                r += k
            sp.dma_start(eps1[:, :], eps_gin.partition_broadcast(P)).then_inc(s_prm, 16)
            sp.dma_start(W1s[:, :, :], W1.rearrange("(k p) n -> p k n", p=P)).then_inc(s_w, 16)
            sp.dma_start(W2s[:, :, :], W2.rearrange("(k p) n -> p k n", p=P)).then_inc(s_w, 16)

            def load_node_tile(c, n=P):
                if at_least(c, 1):
                    sp.wait_ge(s_hx, c)
                sp.dma_start(xt[0:n, :], x[bass.ds(c * P, n), :]).then_inc(s_xt, 16)

            def store_tT(c, b=0):
                sp.wait_ge(s_tb, c + 1)
                sp.dma_start(t_dram[bass.ds(c, 1), :, :].rearrange("c p f -> (c p) f"),
                             tb[b].rearrange("p f n -> p (f n)")).then_inc(s_td, 16)

            def node_tiles(c):
                load_node_tile(c + 1)
                if at_least(c, 1):
                    store_tT(c - 1)

            def load_x(q, rows_=P):
                k, r = q % XU, q // XU
                if r:
                    sp.wait_ge(s_x[k], 16 * r)
                sp.dma_start(x_place(q, rows_),
                             x[q * QN:q * QN + rows_ * 4, :].rearrange("(p b k) d -> p b (k d)", b=2, k=2)
                             ).then_inc(s_x[k], 16)

            load_node_tile(0)
            over(sp, 1, NT - 2, node_tiles)
            load_node_tile(NT - 1, LASTN)
            for q in range(min(X_FIRST, NQF)):
                load_x(q)
            store_tT(NT - 3)

            def load_t(q, k, r, tiles=Q):
                if at_least(q, 2):
                    sp.wait_ge(s_u, FB * (q - 1))
                sp.dma_start(tin[:, k % 2, 0:tiles, :, :].rearrange("p c f n -> p c (f n)"),
                             t_dram[bass.ds(q * Q, tiles), :, :].rearrange("c p f -> p c f")
                             ).then_inc(s_tin[k % 2], 16)

            sp.wait_ge(s_agg, GROUPS)
            sp.wait_ge(s_td, 16 * (NT - 2))
            ahead = min(2, NQF - 1)
            for q in range(ahead):
                load_t(q, q, 0)
            store_tT(NT - 2)
            store_tT(NT - 1, 1)
            sp.wait_ge(s_td, 16 * NT)
            sp.wait_ge(s_bn1, 5)

            def load_both(q, k, r):
                if at_least(q, ahead):
                    load_t(q, k, r)
                if isinstance(q, int):
                    for m in range(X_FIRST + 2 * q, min(X_FIRST + 2 * q + 2, X_EARLY, NQF)):
                        load_x(m)
            chunks(sp, 8, NQF, load_both, lambda q, k, r: load_t(q, k, r, ceil(TAILN, P)))
            last = [NQ - 1 - (NQ - 1 - b) % 2 for b in (0, 1)]
            at_u, at_tin = U_AT // XW, TIN_AT // XW
            for m, s, v in ((at_tin + 2, s_u, FB * (last[1] + 1)),
                            (at_tin, s_u, FB * (last[0] + 1)),
                            (at_u + 2, s_c, last[1] + 1),
                            (at_u, s_c, last[0] + 1)):
                for q in range(m, min(m + 2, NQF)):
                    sp.wait_ge(s, v)
                    load_x(q)
            if TAILN:
                sp.wait_ge(s_rl, DB)
                load_x(NQF, TAILN // 4)

        @block.gpsimd
        def _(pool):
            nc.gpsimd.memset(tab_i[0][:, EB - 1, :], 0).then_inc(s_pad, 1)
            nc.gpsimd.memset(tab_i[1][:, EB - 1, :], N).then_inc(s_pad, 1)
            nc.gpsimd.memset(ident[:, :], 0.0).then_inc(s_ident, 1)
            pool.wait_ge(s_ident, 1)
            nc.gpsimd.affine_select(out=ident[:, :], in_=ident[:, :], compare_op=ALU.not_equal, fill=1.0, base=0,
                                    pattern=[[-1, P]], channel_multiplier=1).then_inc(s_ident, 1)
            nc.gpsimd.iota(sched, pattern=[[P, NI], [0, GI]], base=P * (1 - LAG),
                           channel_multiplier=0).then_inc(s_iota, 1)
            nc.gpsimd.iota(iota_w[:, :], pattern=[[1, W]], base=0, channel_multiplier=0,
                           allow_small_or_imprecise_dtypes=True).then_inc(s_iota, 1)
            nc.gpsimd.memset(aggT[:, :, 0:ZP], 0.0).then_inc(s_zero, 1)

            def gather(i):
                for j in range(GI):
                    g = i * GI + j
                    tiles = tiles_of(i, j)
                    if not tiles:
                        continue
                    if at_least(i, 1):
                        pool.wait_ge(s_h, g - GI + 1)
                    wait_apart(pool, s_idx, g + 1)
                    for k in range(tiles):
                        s = j * GT + k
                        nc.gpsimd.indirect_dma_start(
                            out=rows[:, s, :], out_offset=None, in_=x[:, :],
                            in_offset=bass.IndirectOffsetOnAxis(ap=idx[:, s:s + 1], axis=0)).then_inc(s_rows[j], 16)
            gather(0)
            gather(1)
            pool.wait_ge(s_flag, 1)
            ok = pool.value_load(flag[0:1, 0:1], min_val=0, max_val=1)
            with pool.If(ok < 1):
                nc.gpsimd.iota(g_iota, pattern=[[1, GW]], base=0, channel_multiplier=0,
                               allow_small_or_imprecise_dtypes=True).then_inc(s_iota, 1)
                with pool.Fori(0, TILES) as t:
                    wait_apart(pool, s_gi, t + 1)
                    nc.gpsimd.indirect_dma_start(
                        out=g_row, out_offset=None, in_=x[:, :],
                        in_offset=bass.IndirectOffsetOnAxis(ap=g_idx, axis=0)).then_inc(s_gr, 16)
            with pool.Fori(2, NI - 1) as i:
                gather(i)
            gather(NI - 1)

            def store_out(q, k, r, rows_=P):
                pool.wait_ge(s_sum, q + 1)
                nc.gpsimd.dma_start(out[bass.ds(q * QN, rows_ * 4), :].rearrange("(p b k) d -> p b (k d)", b=2, k=2),
                                    x_place(q, rows_)).then_inc(s_o, 16)
            chunks(pool, XU, NQF, store_out, lambda q, k, r: store_out(q, k, r, TAILN // 4))
            pool.wait_ge(s_o, 16 * NQ)

        @block.vector
        def _(dve):
            V = nc.vector

            def partial_moments(rows_of, stats, s_stats):
                for r, o in zip(rows_of, stats):
                    last = V.bn_stats(o, r)
                last.then_inc(s_stats, 1)

            def moments(stats, mean_var, s_stats, s_mean, v):
                wait_apart(dve, s_stats, v)
                for o, m in zip(stats, mean_var):
                    last = V.bn_aggr(m, o)
                last.then_inc(s_mean, 1)

            def scale_and_shift(mean, std, shift, s_root, s_inv, s_done, v):
                dve.wait_ge(s_root, v)
                V.reciprocal(std, std).then_inc(s_inv, 1)
                dve.wait_ge(s_inv, v)
                V.scalar_tensor_tensor(shift, mean, -1.0, std, ALU.mult, ALU.mult).then_inc(s_done, 1)

            done = [0]

            def own(instruction):
                done[0] += 1
                instruction.then_inc(s_par, 1)
                dve.wait_ge(s_par, done[0])

            def zero_more(at, n):
                return V.tensor_copy(aggT[:, :, ZP + at * ZW:ZP + (at + n) * ZW], aggT[:, :, ZP:ZP + n * ZW])
            own(V.memset(row0, 0.0))
            own(V.memset(row0[0:1, :], 1.0))
            own(V.memset(aggT[:, :, ZP:ZP + ZW], 0.0))
            own(zero_more(1, 1))
            dve.wait_ge(s_first, 16)
            V.tensor_copy(first_f, first_i).then_inc(s_firstf, 1)
            dve.wait_ge(s_firstT, 1)
            V.tensor_copy(idx[:, :], misc_ps[:, 0:SLOTS]).then_inc(s_idx, GI)
            own(zero_more(2, 2))
            own(zero_more(4, 4))
            zero_more(8, 2).then_inc(s_zero, 1)
            dve.wait_ge(s_tab[1], TAB_LOADS)
            V.tensor_copy(tab_f[1], tab_i[1]).then_inc(s_tabf[1], 1)
            zero_more(10, 2).then_inc(s_zero, 1)
            for b in range(NTR):
                w = min(4, EB - 4 * b) * P
                dve.wait_ge(s_tr[1], b + 1)
                V.tensor_copy(dst_f[:, 4 * b * P:4 * b * P + w], tr_ps[1][b % 2][:, 0:w]).then_inc(s_trc[1], 1)

            def statistics(i, j):
                dve.wait_ge(s_rows[j], 64 * i + 16 * tiles_of(i, j))
                partial_moments([rows[:, j * GT + k, :] for k in range(GT)], [st[:, j % 2, k, :] for k in range(GT)],
                                s_bn)

            def mean_and_var(i, j):
                g, r = i * GI + j, j % 2
                if at_least(g, 2):
                    dve.wait_ge(s_h, g - 1)
                moments([st[:, r, k, :] for k in range(GT)], [mv[:, r, k, :] for k in range(GT)], s_bn, s_mv, g + 1)

            def scale(i, j):
                r = j % 2
                scale_and_shift(mv[:, r, :, 0], mv[:, r, :, 1], nb[:, r, :], s_sd, s_rstd, s_st, i * GI + j + 1)

            def selection(i, j):
                g = i * GI + j
                V.tensor_tensor(sel[:, j % 2, :, :],
                                rel[:, bass.ds(g * GT, GT)].unsqueeze(2).to_broadcast([P, GT, W]),
                                iota_w[:, :].unsqueeze(1).to_broadcast([P, GT, W]), ALU.is_equal).then_inc(s_sel, 1)

            def next_rows(i, j):
                V.tensor_copy(idx[:, j * GT:(j + 1) * GT],
                              src_i[:, bass.ds((i + 1) * SLOTS + j * GT, GT)]).then_inc(s_idx, 1)

            statistics(0, 0)
            mean_and_var(0, 0)
            dve.wait_ge(s_base, 1)
            own(V.tensor_scalar(base_f, misc_ps[:, 0:NG], HALF, None, ALU.add))
            dve.wait_ge(s_iota, 2)
            own(V.tensor_tensor(rel_g, dst_f[:, 0:NE].rearrange("p (g k) -> p g k", k=GT),
                                base_f.unsqueeze(2).to_broadcast([P, NG, GT]), ALU.subtract))
            scale(0, 0)
            dve.wait_ge(s_trc[0], NTR)
            next_rows(0, 0)
            own(V.tensor_scalar(iota_w[:, :], iota_w[:, :], -HALF, None, ALU.add))
            selection(0, 0)
            statistics(0, 1)
            mean_and_var(0, 1)
            own(V.tensor_tensor(base_f, base_f, sched, ALU.subtract))
            scale(0, 1)
            next_rows(0, 1)
            selection(0, 1)
            statistics(0, 2)
            mean_and_var(0, 2)
            own(V.tensor_reduce(chk[:, 0:1], rel, X, ALU.max, apply_absolute_value=True))
            own(V.tensor_reduce(chk[:, 1:2], base_f, X, ALU.min))
            own(V.tensor_scalar(chk[:, 2:3], chk[:, 0:1], -1.0, 2 * HALF, ALU.mult, ALU.add))
            V.tensor_reduce(chk[:, 3:4], chk[:, 1:3], X, ALU.min).then_inc(s_pre, 1)
            scale(0, 2)
            next_rows(0, 2)
            dve.wait_ge(s_agg, 1)
            selection(0, 2)
            statistics(0, 3)
            mean_and_var(0, 3)
            dve.wait_ge(s_flagT, 2)
            own(V.tensor_reduce(flag_f[:, :], flag_ps, X, ALU.min))
            V.tensor_scalar(flag[:, :], flag_f[:, :], HALF, None, ALU.is_ge).then_inc(s_flag, 1)
            V.tensor_copy(prmT[:, :], prm_ps).then_inc(s_par, 1)
            V.tensor_scalar(eps1[:, :], eps1[:, :], 1.0, None, ALU.add).then_inc(s_par, 1)
            dve.wait_ge(s_par, done[0] + 2)
            scale(0, 3)
            next_rows(0, 3)
            V.tensor_copy(base_i[:, :], misc_ps[0:1, 0:NG]).then_inc(s_pre, 1)
            dve.wait_ge(s_agg, 2)
            selection(0, 3)
            dve.wait_ge(s_flag, 1)
            ok = dve.value_load(flag[0:1, 0:1], min_val=0, max_val=1)
            dve.wait_ge(s_zero, 6)
            dve.wait_ge(s_pre, 2)

            with dve.If(ok < 1):
                dve.wait_ge(s_iota, 3)
                V.memset(g_nb, 0.0).then_inc(s_gd, 1)
                with dve.Fori(0, TILES) as t:
                    own = t * (4 + 2 * NW) + 1
                    dve.wait_ge(s_gd, own)
                    V.tensor_copy(g_idx, src_i[:, bass.ds(t, 1)]).then_inc(s_gi, 1)
                    V.tensor_copy(g_dst, dst_f[:, bass.ds(t, 1)]).then_inc(s_gd, 1)
                    dve.wait_ge(s_gr, 16 * t + 16)
                    V.bn_stats(g_stat, g_row).then_inc(s_gd, 1)
                    wait_apart(dve, s_gd, own + 2)
                    V.bn_aggr(g_mv, g_stat).then_inc(s_gv, 1)
                    dve.wait_ge(s_gq, t + 1)
                    V.reciprocal(g_mv[:, 1:2], g_mv[:, 1:2]).then_inc(s_gd, 1)
                    dve.wait_ge(s_gd, own + 3)
                    V.scalar_tensor_tensor(g_nb, g_mv[:, 0:1], -1.0, g_mv[:, 1:2], ALU.mult, ALU.mult).then_inc(s_gs, 1)
                    dve.wait_ge(s_gh, t + 1)
                    V.memset(g_nb, 0.0).then_inc(s_gd, 1)
                    with dve.Fori(0, NW) as w:
                        n = t * NW + w
                        dve.wait_ge(s_gd, own + 4 + 2 * w)
                        V.tensor_tensor(g_sel, g_iota, g_dst.to_broadcast([P, GW]), ALU.is_equal).then_inc(s_gm, 1)
                        dve.wait_ge(s_gm, n + 1)
                        V.tensor_scalar(g_dst, g_dst, float(-GW), None, ALU.add).then_inc(s_gd, 1)
                        dve.wait_ge(s_gp, n + 1)
                        z = aggT[:, :, bass.ds(w * GW, GW)]
                        V.tensor_tensor(z, z, g_ps[:, :, 0:GW], ALU.add).then_inc(s_gd, 1)
                V.memset(base_i[:, :], NT * P).then_inc(s_gend, 1)
                dve.wait_ge(s_gend, 1)
                dve.wait_ge(s_gd, TILES * (4 + 2 * NW) + 1)

            def add_window(g, r):
                at = dve.value_load(base_i[0:1, bass.ds(g, 1)], min_val=0, max_val=NT * P)
                dve.wait_ge(s_agg, g + 1)
                if at_least(g, 1):
                    dve.wait_ge(s_add, g)
                z = aggT[:, :, bass.ds(at, W)]
                V.tensor_tensor(z, z, agg_ps[r], ALU.add).then_inc(s_add, 1)

            def statistics_node_tile(c, n=P):
                dve.wait_ge(s_xt, 16 * c + 16)
                partial_moments([xt[0:n, :]], [xst[0:n, :]], s_xbn)

            def mean_and_var_node_tile(c, n=P):
                moments([xst[0:n, :]], [xmv[0:n, :]], s_xbn, s_xmv, c + 1)

            def scale_node_tile(c, n=P):
                scale_and_shift(xmv[0:n, 0:1], xmv[0:n, 1:2], xnb[0:n, :], s_xsd, s_xrs, s_xst, c + 1)

            def z_tile(c, added, n=P, b=0, hb=0):
                dve.wait_ge(s_hT, c + 1)
                dve.wait_ge(s_add, added)
                if at_least(c, 1) and b == 0:
                    dve.wait_ge(s_t, c)
                V.scalar_tensor_tensor(zt[b][:, :, 0:n], hT_ps[hb][:, :, 0:n], eps1[:, 0:1],
                                       aggT[:, :, bass.ds(c * P, n)], ALU.mult, ALU.add).then_inc(s_zt, 1)

            def t_stats(c, n=P, b=0):
                dve.wait_ge(s_tb, c + 1)
                for f in range(FB):
                    last = V.bn_stats(st1[:, f, bass.ds(c * 6, 6)], tb[b][:, f, 0:n])
                last.then_inc(s_tst, 1)

            def iteration(i):
                a, c = i - LAG + 1, i - LAG
                for j in range(GI):
                    if not tiles_of(i, j):
                        continue
                    statistics(i, j)
                    if at_least(a, 0) and j == 0:
                        statistics_node_tile(a)
                    add_window(i * GI + j - 2, j % 2)
                    mean_and_var(i, j)
                    if at_least(a, 0) and j == 0:
                        mean_and_var_node_tile(a)
                    selection(i, j)
                    if not isinstance(i, int) or i < NI - 1:
                        next_rows(i, j)
                    if at_least(c, 1) and j == 1:
                        t_stats(c - 1)
                    scale(i, j)
                    if at_least(a, 0) and j == 0:
                        scale_node_tile(a)
                    if at_least(c, 0) and j == 1:
                        z_tile(c, i * GI)
            add_window(0, 0)
            add_window(1, 1)
            iteration(1)
            iteration(2)
            with dve.Fori(LAG + 1, NI - 1) as i:
                iteration(i)
            iteration(NI - 1)
            statistics_node_tile(NT - 1, LASTN)
            mean_and_var_node_tile(NT - 1, LASTN)
            V.memset(tb[1], 0.0)
            add_window(GROUPS - 2, GROUPS % 2)
            scale_node_tile(NT - 1, LASTN)
            add_window(GROUPS - 1, (GROUPS - 1) % 2)
            z_tile(NT - 2, GROUPS, P, 0, 1)
            t_stats(NT - 3)
            z_tile(NT - 1, GROUPS, LASTN, 1, 2)
            t_stats(NT - 2)
            t_stats(NT - 1, LASTN, 1)

            def batch_norm(stats_, mean_var, gT, btT, scale, shift, tmp, blocks, s_own, s_root, s_stats, v):
                dve.wait_ge(s_stats, v)
                for f in range(blocks):
                    last = V.bn_aggr(mean_var[:, f, :], stats_[:, f, :])
                last.then_inc(s_own, 1)
                dve.wait_ge(s_root, 1)
                V.reciprocal(tmp[:, :], tmp[:, :]).then_inc(s_own, 1)
                dve.wait_ge(s_own, 2)
                V.tensor_tensor(scale[:, :], tmp[:, :], gT, ALU.mult).then_inc(s_own, 1)
                dve.wait_ge(s_own, 3)
                V.tensor_tensor(tmp[:, :], mean_var[:, :, 0], scale[:, :], ALU.mult).then_inc(s_own, 1)
                dve.wait_ge(s_own, 4)
                V.tensor_tensor(shift[:, :], btT, tmp[:, :], ALU.subtract).then_inc(s_own, 1)
            batch_norm(st1, mv1, g1T, bt1T, sc1, sh1, tmp1, FB, s_bn1, s_root1, s_tst, NT)

            def y_chunk(q, k, r, n=QN):
                dve.wait_ge(s_c, q + 1)
                for f in range(DB):
                    y = aggT[:, f, bass.ds(q * QN, n)]
                    last = V.scalar_tensor_tensor(y, c_ps[k % 2][f][:, 0:n], b2T[:, f:f + 1], y, ALU.add, ALU.add)
                last.then_inc(s_y, 1)
                dve.wait_ge(s_y, q + 1)
                for f in range(DB):
                    last = V.bn_stats(st2[:, f, bass.ds(q * 6, 6)], aggT[:, f, bass.ds(q * QN, n)])
                last.then_inc(s_yst, 1)
            chunks(dve, 4, NQF, y_chunk, lambda q, k, r: y_chunk(q, k, r, TAILN))
            batch_norm(st2, mv2, g2T, bt2T, sc2, sh2, tmp2, DB, s_bn2, s_root2, s_yst, NQ)

            def residual(q, k, r, rows_=P):
                dve.wait_ge(s_x[k], 16 * r + 16)
                dve.wait_ge(s_oT, q + 1)
                V.tensor_tensor(x_place(q, rows_), o_ps[k % 2][0:rows_, :, :],
                                x_place(q, rows_), ALU.add).then_inc(s_sum, 1)
            chunks(dve, XU, NQF, residual, lambda q, k, r: residual(q, k, r, TAILN // 4))

        @block.scalar
        def _(act):
            S = nc.scalar
            act.preload_act_table(ACT.Sqrt)

            def zero_step(n):
                S.memzero(aggT[:, :, ZA[n]:ZA[n + 1]]).then_inc(s_zero, 1)
            zero_step(0)
            act.wait_ge(s_tab[0], TAB_LOADS)
            S.copy(tab_f[0], tab_i[0]).then_inc(s_tabf[0], 1)
            zero_step(1)
            for b in range(NTR):
                w = min(4, EB - 4 * b) * P
                act.wait_ge(s_tr[0], b + 1)
                S.copy(src_i[:, 4 * b * P:4 * b * P + w], tr_ps[0][b % 2][:, 0:w]).then_inc(s_trc[0], 1)

            def root(i, j):
                act.wait_ge(s_mv, i * GI + j + 1)
                var = mv[:, j % 2, :, 1]
                S.activation(var, var, ACT.Sqrt, bias=LN_EPS).then_inc(s_sd, 1)

            def root_node_tile(c, n=P):
                act.wait_ge(s_xmv, c + 1)
                S.activation(xmv[0:n, 1:2], xmv[0:n, 1:2], ACT.Sqrt, bias=LN_EPS).then_inc(s_xsd, 1)

            def normalise(i, j):
                g, r = i * GI + j, j % 2
                act.wait_ge(s_st, g + 1)
                if at_least(g, 2):
                    act.wait_ge(s_agg, g - 1)
                for k in range(GT):
                    last = S.activation(hrow[:, r, k, :], rows[:, j * GT + k, :], ACT.Relu,
                                        bias=nb[:, r, k:k + 1], scale=mv[:, r, k, 1:2])
                last.then_inc(s_h, 1)

            def norm_node_tile(c, n=P):
                act.wait_ge(s_xst, c + 1)
                if at_least(c, 1):
                    act.wait_ge(s_hT, c)
                S.activation(hx[0:n, :], xt[0:n, :], ACT.Relu, bias=xnb[0:n, :], scale=xmv[0:n, 1:2]).then_inc(s_hx, 1)

            def keep_hT(c, n=P, hb=0):
                act.wait_ge(s_zt, c + 1)
                S.copy(aggT[:, :, bass.ds(c * P, n)], hT_ps[hb][:, :, 0:n]).then_inc(s_hTc, 1)

            def t_and_b1(c, n=P, b=0):
                act.wait_ge(s_t, c + 1)
                if at_least(c, 1) and b == 0:
                    act.wait_ge(s_td, 16 * c)
                    act.wait_ge(s_tst, c)
                for f in range(FB):
                    last = S.activation(tb[b][:, f, 0:n], t_ps[b][:, f, 0:n], ACT.Identity, bias=b1T[:, f:f + 1],
                                        scale=1.0)
                last.then_inc(s_tb, 1)

            for j in range(GI):
                root(0, j)
                if j == 2:
                    zero_step(2)
                normalise(0, j)
            act.wait_ge(s_flag, 1)
            ok = act.value_load(flag[0:1, 0:1], min_val=0, max_val=1)
            with act.If(ok < 1):
                with act.Fori(0, TILES) as t:
                    act.wait_ge(s_gv, t + 1)
                    S.activation(g_mv[:, 1:2], g_mv[:, 1:2], ACT.Sqrt, bias=LN_EPS).then_inc(s_gq, 1)
                    act.wait_ge(s_gs, t + 1)
                    S.activation(g_h, g_row, ACT.Relu, bias=g_nb, scale=g_mv[:, 1:2]).then_inc(s_gh, 1)
                act.wait_ge(s_gend, 1)

            def iteration(i):
                a, c = i - LAG + 1, i - LAG
                for j in range(GI):
                    if not tiles_of(i, j):
                        continue
                    root(i, j)
                    if at_least(a, 0) and j == 0:
                        root_node_tile(a)
                    normalise(i, j)
                    if at_least(a, 0) and j == 0:
                        norm_node_tile(a)
                    if at_least(c, 0) and j == 2:
                        keep_hT(c)
                if isinstance(i, int) and i == NI - 1:
                    root_node_tile(NT - 1, LASTN)
                    norm_node_tile(NT - 1, LASTN)
                if at_least(c, 0):
                    t_and_b1(c)
            iteration(1)
            iteration(2)
            with act.Fori(LAG + 1, NI - 1) as i:
                iteration(i)
            iteration(NI - 1)
            keep_hT(NT - 2, P, 1)
            keep_hT(NT - 1, LASTN, 2)
            t_and_b1(NT - 2)
            t_and_b1(NT - 1, LASTN, 1)

            def batch_root(mean_var, tmp, s_own, s_root):
                act.wait_ge(s_own, 1)
                S.activation(tmp[:, :], mean_var[:, :, 1], ACT.Sqrt, bias=BN_EPS).then_inc(s_root, 1)
            batch_root(mv1, tmp1, s_bn1, s_root1)
            act.wait_ge(s_bn1, 5)

            def relu1(q, k, r, tiles=Q):
                act.wait_ge(s_tin[k % 2], 32 * r + 16 * (k // 2) + 16)
                if at_least(q, 2):
                    act.wait_ge(s_c, q - 1)
                for f in range(FB):
                    S.activation(u[:, k % 2, f, 0:tiles * P].rearrange("p (c n) -> p c n", n=P),
                                 tin[:, k % 2, 0:tiles, f, :], ACT.Relu, bias=sh1[:, f:f + 1],
                                 scale=sc1[:, f:f + 1]).then_inc(s_u, 1)
            chunks(act, 4, NQF, relu1, lambda q, k, r: relu1(q, k, r, ceil(TAILN, P)))
            batch_root(mv2, tmp2, s_bn2, s_root2)
            act.wait_ge(s_bn2, 5)

            def relu2(q, k, r, n=QN):
                if at_least(q, 2):
                    act.wait_ge(s_oT, q - 1)
                for f in range(DB):
                    S.activation(rl[k % 2][:, f, 0:n], aggT[:, f, bass.ds(q * QN, n)], ACT.Relu,
                                 bias=sh2[:, f:f + 1], scale=sc2[:, f:f + 1]).then_inc(s_rl, 1)
            chunks(act, XU, NQF, relu2, lambda q, k, r: relu2(q, k, r, TAILN))

        @block.tensor
        def _(pe):
            T = nc.tensor
            pe.wait_ge(s_ident, 2)
            pe.wait_ge(s_firstf, 1)
            T.transpose(misc_ps[:, 0:SLOTS], first_f, ident[0:SLOTS, 0:SLOTS]).then_inc(s_firstT, 1)

            def table(n, banks):
                pe.wait_ge(s_tabf[n], 1)
                for b in banks:
                    if b >= 2:
                        pe.wait_ge(s_trc[n], b - 1)
                    for m in range(min(4, EB - 4 * b)):
                        last = T.transpose(tr_ps[n][b % 2][:, m * P:(m + 1) * P], tab_f[n][:, 4 * b + m, :],
                                           ident[:, :])
                    last.then_inc(s_tr[n], 1)
            table(1, range(NTR))
            table(0, range(1))
            pe.wait_ge(s_trc[1], NTR)
            pe.wait_ge(s_par, 2)
            T.matmul(misc_ps[:, 0:NG], row0, dst_f[:, 0:NE:GT], start=True, stop=True).then_inc(s_base, 1)
            table(0, range(1, NTR))

            def aggregate(i, j):
                g, r = i * GI + j, j % 2
                pe.wait_ge(s_h, g + 1)
                pe.wait_ge(s_sel, g + 1)
                if at_least(g, 2):
                    pe.wait_ge(s_add, g - 1)
                for f in range(DB):
                    for k in range(GT):
                        last = T.matmul(agg_ps[r][:, f, :], hrow[:, r, k, f * P:(f + 1) * P], sel[:, r, k, :],
                                        start=k == 0, stop=k == GT - 1)
                last.then_inc(s_agg, 1)

            def transpose_h(c, n=P, hb=0):
                pe.wait_ge(s_hx, c + 1)
                if at_least(c, 1) and hb == 0:
                    pe.wait_ge(s_hTc, c)
                for f in range(DB):
                    last = T.transpose(hT_ps[hb][:, f, 0:n], hx[0:n, f * P:(f + 1) * P], ident[0:n, 0:n])
                last.then_inc(s_hT, 1)

            def times_W1(c, n=P, b=0):
                pe.wait_ge(s_zt, c + 1)
                if at_least(c, 1) and b == 0:
                    pe.wait_ge(s_tb, c)
                for m in range(FB):
                    for k in range(DB):
                        last = T.matmul(t_ps[b][:, m, 0:n], W1s[:, k, m * P:(m + 1) * P], zt[b][:, k, 0:n],
                                        start=k == 0, stop=k == DB - 1)
                last.then_inc(s_t, 1)

            aggregate(0, 0)
            aggregate(0, 1)
            pe.wait_ge(s_prm, 16 * 7)
            T.transpose(prm_ps, prm[:, :], ident[0:18, 0:18]).then_inc(s_flagT, 1)
            pe.wait_ge(s_pre, 1)
            T.transpose(flag_ps, chk[:, 3:4], ident[:, :]).then_inc(s_flagT, 1)
            pe.wait_ge(s_flag, 1)
            ok = pe.value_load(flag[0:1, 0:1], min_val=0, max_val=1)
            with pe.If(ok < 1):
                with pe.Fori(0, TILES) as t:
                    wait_apart(pe, s_gh, t + 1)
                    with pe.Fori(0, NW) as w:
                        pe.wait_ge(s_gm, t * NW + w + 1)
                        for f in range(DB):
                            last = T.matmul(g_ps[:, f, 0:GW], g_h[:, f * P:(f + 1) * P], g_sel, start=True, stop=True)
                        last.then_inc(s_gp, 1)
                pe.wait_ge(s_gend, 1)

            def iteration(i):
                a, c = i - LAG + 1, i - LAG
                for j in range(GI):
                    if not tiles_of(i, j):
                        continue
                    last = isinstance(i, int) and i == NI - 1
                    if at_least(c, 0) and j == 0:
                        transpose_h(c)
                    if last and j == 1:
                        times_W1(c)
                    aggregate(i, j)
                    if last and j == 1:
                        transpose_h(NT - 2, P, 1)
                    if at_least(c, 0) and j == 1 and not last:
                        times_W1(c)
            pe.wait_ge(s_w, 32)
            aggregate(0, 2)
            aggregate(0, 3)
            iteration(1)
            iteration(2)
            with pe.Fori(LAG + 1, NI - 1) as i:
                iteration(i)
            iteration(NI - 1)
            transpose_h(NT - 1, LASTN, 2)
            times_W1(NT - 2)
            times_W1(NT - 1, LASTN, 1)

            def keep_warm(n):
                for _ in range(n):
                    T.matmul(ps[:, 7, 0:P], ident[:, :], ident[:, :], start=True, stop=True)
            keep_warm(26)

            def times_W2(q, k, r, n=QN):
                if at_least(q, 2):
                    pe.wait_ge(s_y, q - 1)
                for m in range(DB):
                    for f in range(FB):
                        if m == 0:
                            pe.wait_ge(s_u, FB * q + f + 1)
                        last = T.matmul(c_ps[k % 2][m][:, 0:n], W2s[:, f, m * P:(m + 1) * P], u[:, k % 2, f, 0:n],
                                        start=f == 0, stop=f == FB - 1)
                last.then_inc(s_c, 1)
            chunks(pe, 4, NQF, times_W2, lambda q, k, r: times_W2(q, k, r, TAILN))
            keep_warm(16)

            def transpose_out(q, k, r, n=QN):
                if at_least(q, 2):
                    pe.wait_ge(s_sum, q - 1)
                for f in range(DB):
                    pe.wait_ge(s_rl, DB * q + f + 1)
                    for m in range(4):
                        at = (m % 2) * D + f * P
                        last = T.transpose(o_ps[k % 2][0:n // 4, m // 2, at:at + P],
                                           rl[k % 2][:, f, m:n:4], ident[:, :])
                last.then_inc(s_oT, 1)
            chunks(pe, XU, NQF, transpose_out, lambda q, k, r: transpose_out(q, k, r, TAILN))


_INS = ["x", "src", "dst", "L0_gnn_W1", "L0_gnn_b1", "L0_gnn_g1", "L0_gnn_bt1", "L0_gnn_W2", "L0_gnn_b2",
        "L0_gnn_g2", "L0_gnn_bt2", "L0_gnn_eps_gin"]


def kernel(**inputs):
    import numpy as np
    import concourse.bacc as bacc
    from concourse.bass_utils import run_bass_kernel_spmd

    nc = bacc.Bacc("TRN2", target_bir_lowering=False, num_devices=1)
    arrays, args = {}, []
    for name in _INS:
        a = np.ascontiguousarray(inputs[name])
        if name.endswith("eps_gin"):
            a = a.reshape(1, 1)
        arrays[f"in_{name}"] = a
        args.append(nc.dram_tensor(f"in_{name}", a.shape, mybir.dt.from_np(a.dtype), kind="ExternalInput").ap())
    out = nc.dram_tensor("out", inputs["x"].shape, mybir.dt.float32, kind="ExternalOutput").ap()
    build(nc, *args, out)
    r = run_bass_kernel_spmd(nc, [arrays], core_ids=[0])
    return r.results[0]["out"]
```
